# Optimizing a Trainium2 kernel written in Bass

```python
import numpy as np
import jax
import jax.numpy as jnp

def _softmax(x, axis=-1):
    return jax.nn.softmax(x, axis=axis)

def _gelu(x):
    return jax.nn.gelu(x, approximate=True)

def _silu(x):
    return jax.nn.silu(x)

def _sigmoid(x):
    return jax.nn.sigmoid(x)

def _layernorm(x, axis=-1, eps=1e-05):
    m = jnp.mean(x, axis=axis, keepdims=True)
    v = jnp.var(x, axis=axis, keepdims=True)
    return (x - m) / jnp.sqrt(v + eps)

def _scatter_add(tgt, idx, src, axis=0):
    return tgt.at[idx].add(src)

def _segment_sum(src, seg, n):
    return jax.ops.segment_sum(src, seg, n)
kernel_name = 'mk_vit_tower_d1_tok_img1024_r4_d8f67f'

def setup_inputs(seed: int=0):
    np.random.seed(seed)
    _w = jnp.asarray

    def _rec_inputs():
        import jax
        import jax.numpy as jnp
        _rk = jax.random.key(seed)
        x = -0.00016672 + 0.999947 * jax.random.normal(jax.random.fold_in(_rk, 1), (16, 3, 96, 96), jnp.float32)
        return x
    x = _rec_inputs()

    def _L0_tok_setup():
        import jax, jax.numpy as jnp
        import numpy as np
        P = 16

        def _patchify(x):
            B, C, H, W = x.shape
            gh, gw = (H // P, W // P)
            x = x.reshape(B, C, gh, P, gw, P)
            x = x.transpose(0, 2, 4, 1, 3, 5)
            return x.reshape(B, gh * gw, C * P * P)
        key = jax.random.key(seed)
        k1, k2, k3, k4, k5 = jax.random.split(key, 5)
        B, C, S = (64, 3, 96)
        lin_in, lout = (P * P * C, 256)
        n_patches = (S // P) ** 2
        return {'x': jax.random.normal(k1, (B, C, S, S), dtype=jnp.float32), 'W': jax.random.normal(k2, (lout, lin_in), dtype=jnp.float32) * 0.02, 'b': jax.random.normal(k3, (lout,), dtype=jnp.float32) * 0.02, 'class_token': jax.random.normal(k4, (1, 1, lout), dtype=jnp.float32) * 0.02, 'pos_embedding': jax.random.normal(k5, (1, n_patches + 1, lout), dtype=jnp.float32) * 0.02}
    _L0_tok_all = _L0_tok_setup()
    _L0_tok_in = {k: v for k, v in _L0_tok_all.items() if k in ('W', 'b', 'class_token', 'pos_embedding')}
    del _L0_tok_all

    def _L0_attn_setup():
        import jax, jax.numpy as jnp
        import numpy as np
        from math import sqrt
        HEADS = 16
        MODEL_DIM = 256
        DIM_PER_HEAD = MODEL_DIM // HEADS
        MAX_REL_POS = 32
        ROPE_BASE = 10000.0
        NEG_INF = -1e+18

        def _rope_cos_sin(seq_len, dim):
            inv_freq = 1.0 / ROPE_BASE ** (jnp.arange(0, dim, 2, dtype=jnp.float32) / dim)
            t = jnp.arange(seq_len, dtype=jnp.float32)
            ang = jnp.outer(t, inv_freq)
            return (jnp.cos(ang), jnp.sin(ang))

        def _apply_rotary_interleave(x, cos, sin):
            B, H, L, D = x.shape
            x_ = x.reshape(B, H, L, D // 2, 2)
            xe, xo = (x_[..., 0], x_[..., 1])
            c = cos[None, None, :, :]
            s = sin[None, None, :, :]
            oe = xe * c - xo * s
            oo = xe * s + xo * c
            return jnp.stack([oe, oo], axis=-1).reshape(B, H, L, D)
        key = jax.random.key(seed)
        ks = jax.random.split(key, 6)
        B, L = (2, 256)
        scale = 0.02
        x = jax.random.normal(ks[0], (B, L, MODEL_DIM), dtype=jnp.float32)
        w_q = jax.random.normal(ks[1], (MODEL_DIM, MODEL_DIM), dtype=jnp.float32) * scale
        w_k = jax.random.normal(ks[2], (MODEL_DIM, MODEL_DIM), dtype=jnp.float32) * scale
        w_v = jax.random.normal(ks[3], (MODEL_DIM, MODEL_DIM), dtype=jnp.float32) * scale
        w_o = jax.random.normal(ks[4], (MODEL_DIM, MODEL_DIM), dtype=jnp.float32) * scale
        rel_emb = jax.random.normal(ks[5], (2 * MAX_REL_POS + 1, DIM_PER_HEAD), dtype=jnp.float32) * scale
        return {'x': x, 'w_q': w_q, 'w_k': w_k, 'w_v': w_v, 'w_o': w_o, 'rel_emb': rel_emb}
    _L0_attn_all = _L0_attn_setup()
    _L0_attn_in = {k: v for k, v in _L0_attn_all.items() if k in ('w_q', 'w_k', 'w_v', 'w_o', 'rel_emb')}
    del _L0_attn_all

    def _L0_ffn_setup():
        import jax, jax.numpy as jnp
        import numpy as np
        E = 32
        H = 256
        I = 128
        G = 8
        TKG = 4
        TOPK = 8
        NSH = 2
        SCALE = 2.5
        key = jax.random.key(seed)
        ks = jax.random.split(key, 10)
        s = 0.02
        return {'hidden_states': jax.random.normal(ks[0], (2, 256, H), jnp.float32), 'gate_w': jax.random.normal(ks[1], (E, H), jnp.float32) * s, 'gate_bias': jax.random.normal(ks[2], (E,), jnp.float32) * s, 'w_gate': jax.random.normal(ks[3], (E, I, H), jnp.float32) * s, 'w_up': jax.random.normal(ks[4], (E, I, H), jnp.float32) * s, 'w_down': jax.random.normal(ks[5], (E, H, I), jnp.float32) * s, 'sh_gate': jax.random.normal(ks[6], (I * NSH, H), jnp.float32) * s, 'sh_up': jax.random.normal(ks[7], (I * NSH, H), jnp.float32) * s, 'sh_down': jax.random.normal(ks[8], (H, I * NSH), jnp.float32) * s}
    _L0_ffn_all = _L0_ffn_setup()
    _L0_ffn_in = {k: v for k, v in _L0_ffn_all.items() if k in ('gate_w', 'gate_bias', 'w_gate', 'w_up', 'w_down', 'sh_gate', 'sh_up', 'sh_down')}
    del _L0_ffn_all
    return {'x': x, 'L0_tok_W': _L0_tok_in['W'], 'L0_tok_b': _L0_tok_in['b'], 'L0_tok_class_token': _L0_tok_in['class_token'], 'L0_tok_pos_embedding': _L0_tok_in['pos_embedding'], 'L0_attn_w_q': _L0_attn_in['w_q'], 'L0_attn_w_k': _L0_attn_in['w_k'], 'L0_attn_w_v': _L0_attn_in['w_v'], 'L0_attn_w_o': _L0_attn_in['w_o'], 'L0_attn_rel_emb': _L0_attn_in['rel_emb'], 'L0_ffn_gate_w': _L0_ffn_in['gate_w'], 'L0_ffn_gate_bias': _L0_ffn_in['gate_bias'], 'L0_ffn_w_gate': _L0_ffn_in['w_gate'], 'L0_ffn_w_up': _L0_ffn_in['w_up'], 'L0_ffn_w_down': _L0_ffn_in['w_down'], 'L0_ffn_sh_gate': _L0_ffn_in['sh_gate'], 'L0_ffn_sh_up': _L0_ffn_in['sh_up'], 'L0_ffn_sh_down': _L0_ffn_in['sh_down']}

def reference(x, L0_tok_W, L0_tok_b, L0_tok_class_token, L0_tok_pos_embedding, L0_attn_w_q, L0_attn_w_k, L0_attn_w_v, L0_attn_w_o, L0_attn_rel_emb, L0_ffn_gate_w, L0_ffn_gate_bias, L0_ffn_w_gate, L0_ffn_w_up, L0_ffn_w_down, L0_ffn_sh_gate, L0_ffn_sh_up, L0_ffn_sh_down):
    import jax
    import jax.numpy as jnp

    def _L0_tok_ref(x, W, b, class_token, pos_embedding):
        import jax, jax.numpy as jnp
        import numpy as np
        P = 16

        def _patchify(x):
            B, C, H, W = x.shape
            gh, gw = (H // P, W // P)
            x = x.reshape(B, C, gh, P, gw, P)
            x = x.transpose(0, 2, 4, 1, 3, 5)
            return x.reshape(B, gh * gw, C * P * P)
        patches = _patchify(x)
        proj = jnp.einsum('bnk,dk->bnd', patches, W) + b
        B = x.shape[0]
        cls = jnp.broadcast_to(class_token, (B, 1, proj.shape[-1]))
        out = jnp.concatenate([cls, proj], axis=1) + pos_embedding
        return out

    def _L0_attn_ref(x, w_q, w_k, w_v, w_o, rel_emb):
        import jax, jax.numpy as jnp
        import numpy as np
        from math import sqrt
        HEADS = 16
        MODEL_DIM = 256
        DIM_PER_HEAD = MODEL_DIM // HEADS
        MAX_REL_POS = 32
        ROPE_BASE = 10000.0
        NEG_INF = -1e+18

        def _rope_cos_sin(seq_len, dim):
            inv_freq = 1.0 / ROPE_BASE ** (jnp.arange(0, dim, 2, dtype=jnp.float32) / dim)
            t = jnp.arange(seq_len, dtype=jnp.float32)
            ang = jnp.outer(t, inv_freq)
            return (jnp.cos(ang), jnp.sin(ang))

        def _apply_rotary_interleave(x, cos, sin):
            B, H, L, D = x.shape
            x_ = x.reshape(B, H, L, D // 2, 2)
            xe, xo = (x_[..., 0], x_[..., 1])
            c = cos[None, None, :, :]
            s = sin[None, None, :, :]
            oe = xe * c - xo * s
            oo = xe * s + xo * c
            return jnp.stack([oe, oo], axis=-1).reshape(B, H, L, D)
        B, L, _ = x.shape

        def shape(t):
            return t.reshape(B, L, HEADS, DIM_PER_HEAD).transpose(0, 2, 1, 3)
        q = shape(x @ w_q.T)
        k = shape(x @ w_k.T)
        v = shape(x @ w_v.T)
        cos, sin = _rope_cos_sin(L, DIM_PER_HEAD)
        q = _apply_rotary_interleave(q, cos, sin)
        k = _apply_rotary_interleave(k, cos, sin)
        q = q / sqrt(DIM_PER_HEAD)
        scores = jnp.einsum('bhqd,bhkd->bhqk', q, k)
        pos = jnp.arange(L)
        rel_idx = jnp.clip(pos[None, :] - pos[:, None], -MAX_REL_POS, MAX_REL_POS) + MAX_REL_POS
        rel = rel_emb[rel_idx]
        scores = scores + jnp.einsum('bhqd,qkd->bhqk', q, rel)
        causal = jnp.tril(jnp.ones((L, L), dtype=bool))
        scores = jnp.where(causal[None, None], scores, NEG_INF)
        attn = jax.nn.softmax(scores, axis=-1)
        ctx = jnp.einsum('bhqk,bhkd->bhqd', attn, v)
        ctx = ctx + jnp.einsum('bhqk,qkd->bhqd', attn, rel)
        out = ctx.transpose(0, 2, 1, 3).reshape(B, L, MODEL_DIM) @ w_o.T
        return out

    def _L0_ffn_ref(hidden_states, gate_w, gate_bias, w_gate, w_up, w_down, sh_gate, sh_up, sh_down):
        import jax, jax.numpy as jnp
        import numpy as np
        E = 32
        H = 256
        I = 128
        G = 8
        TKG = 4
        TOPK = 8
        NSH = 2
        SCALE = 2.5
        B, S, Hd = hidden_states.shape
        h = hidden_states.reshape(-1, Hd)
        logits = h.astype(jnp.float32) @ gate_w.T
        scores = jax.nn.sigmoid(logits)
        sc = scores + gate_bias
        grp = sc.reshape(-1, G, E // G)
        group_scores = jax.lax.top_k(grp, 2)[0].sum(-1)
        gidx = jax.lax.top_k(group_scores, TKG)[1]
        gmask = jnp.sum(jax.nn.one_hot(gidx, G, dtype=sc.dtype), axis=1)
        smask = jnp.repeat(gmask, E // G, axis=1)
        masked = jnp.where(smask > 0, sc, jnp.zeros_like(sc))
        tki = jax.lax.top_k(masked, TOPK)[1]
        tkw = jnp.take_along_axis(scores, tki, axis=1)
        tkw = tkw / (tkw.sum(-1, keepdims=True) + 1e-20)
        tkw = tkw * SCALE
        combine = (jax.nn.one_hot(tki, E, dtype=tkw.dtype) * tkw[..., None]).sum(1)
        g = jax.nn.silu(jnp.einsum('th,eih->tei', h, w_gate))
        u = jnp.einsum('th,eih->tei', h, w_up)
        routed = jnp.einsum('tei,ehi->th', g * u * combine[:, :, None], w_down)
        sg = jax.nn.silu(h @ sh_gate.T)
        shared = sg * (h @ sh_up.T) @ sh_down.T
        return (routed + shared).reshape(B, S, Hd)
    h = _L0_tok_ref(x, L0_tok_W, L0_tok_b, L0_tok_class_token, L0_tok_pos_embedding)
    h = h + _L0_attn_ref(_layernorm(h, axis=-1), L0_attn_w_q, L0_attn_w_k, L0_attn_w_v, L0_attn_w_o, L0_attn_rel_emb)
    h = h + _L0_ffn_ref(_layernorm(h, axis=-1), L0_ffn_gate_w, L0_ffn_gate_bias, L0_ffn_w_gate, L0_ffn_w_up, L0_ffn_w_down, L0_ffn_sh_gate, L0_ffn_sh_up, L0_ffn_sh_down)
    return h

_drawn_inputs = setup_inputs


def setup_inputs(seed=0):
    import zlib

    import numpy as np

    out = dict(_drawn_inputs(seed))
    spreads = {}
    factors = {'L0_attn_w_q': 8.0,
     'L0_attn_w_k': 8.0,
     'L0_attn_rel_emb': 8.0,
     'L0_ffn_gate_w': 3.453,
     'L0_ffn_gate_bias': 6.783,
     'L0_ffn_w_gate': 2.96,
     'L0_ffn_w_up': 2.927,
     'L0_ffn_w_down': 2.916}
    for name, (base, spread) in spreads.items():
        noise = np.random.default_rng([zlib.crc32(name.encode()), seed]).standard_normal(out[name].shape)
        drawn = base * np.exp(spread * noise) if base else spread * noise
        out[name] = jnp.asarray(drawn.astype(out[name].dtype))
    for name, factor in factors.items():
        out[name] = (out[name] * factor).astype(out[name].dtype)
    return out
```

```python
from contextlib import ExitStack

import numpy as np

import concourse.bass as bass
from concourse import mybir

F32 = mybir.dt.float32
F32R = mybir.dt.float32r
ALU = mybir.AluOpType
ACT = mybir.ActivationFunctionType
AX_X = mybir.AxisListType.X

B, L, D = 16, 37, 256
NP = L - 1
T = B * L
KP = 768 // 128
MC = D // 128
HB = B // 2
TH = HB * L
TP = HB * NP
HD = 16
E, INTER = 32, 128
NSH = 2
G, GE, TKG, TOPK = 8, 4, 4, 8
SCALE = 2.5
NEG = -1e18
EPS = 1e-5

IPS = 4
NSTEP = MC * B // IPS
PAIR = 2 * L
CH = 4 * IPS
GRP = 2
NG = NSTEP // GRP
CG = GRP * CH
ZW = 2 * L - 1
YW = 3 * L - 1

NE = NSH + E
RING = 4
WE = 3 * 2 * 128

C_BIAS = 0
C_CLS = C_BIAS + MC
C_POS = C_CLS + MC
C_COS = C_POS + MC * L
C_SIN = C_COS + L
C_QM = C_SIN + L
C_OM = C_QM + 2
C_REL = C_OM + 2
C_GW = C_REL + L
C_GB = C_GW + MC * E
C_LOW = C_GB + E
C_EPS = C_LOW + G * G
C_ONE = C_EPS + 1
C_ID = C_ONE + 128
C_ALL = C_ID + 128


def build(nc, emb, cst, rel_v, wattn, wexp, out):
    zd = nc.dram_tensor("rel_scores", (PAIR, NSTEP * CH, ZW), F32)
    yd = nc.dram_tensor("probs", (PAIR, NSTEP * CH, YW), F32)
    cd = nc.dram_tensor("combine", (E, T), F32).ap()

    with ExitStack() as ctx:
        def sem(name):
            return ctx.enter_context(nc.semaphore(name))

        def sb(name, shape, dt=F32, scope=ctx):
            return scope.enter_context(nc.sbuf_tensor(name, shape, dt))

        ps = ctx.enter_context(nc.psum_tensor("ps", [128, 8, 512], F32))

        cs = sb("cs", [128, C_ALL])
        hT = sb("hT", [128, MC, T])
        dT = sb("dT", [128, MC, T])
        sq = sb("sq", [128, MC, T])
        sd = sb("sd", [128, T])
        rs = sb("rs", [128, T])
        xn = sb("xn", [128, MC, T])
        wst = sb("wst", [128, RING, WE])
        whi = sb("whi", [128, RING, WE], F32R)
        wlo = sb("wlo", [128, RING, WE], F32R)

        attn = ExitStack()
        wat = sb("wat", [128, 4, MC, D], F32, attn)
        qk = sb("qk", [128, 2, MC, T], F32, attn)
        qksw = sb("qksw", [128, 2, T], F32, attn)
        qkc = sb("qkc", [128, 2, T], F32, attn)
        qrot = sb("qrot", [128, MC, T], F32, attn)
        qbd = sb("qbd", [128, MC, B, PAIR], F32, attn)
        ke = sb("ke", [128, MC, B, PAIR], F32, attn)
        ve = sb("ve", [PAIR, B, D], F32, attn)
        zb = sb("zb", [PAIR, 2, CG, ZW], F32, attn)
        sc = sb("sc", [PAIR, 2, CG, L], F32, attn)
        rl = sb("rl", [PAIR, 2, CG, L], F32, attn)
        st_mx = sb("st_mx", [PAIR, CG], F32, attn)
        st_sum = sb("st_sum", [PAIR, CG], F32, attn)
        st_inv = sb("st_inv", [PAIR, CG], F32, attn)
        pt = sb("pt", [PAIR, 4, CH // 2, PAIR], F32, attn)
        cth = sb("cth", [128, 2, IPS, L], F32, attn)
        ctxT = sb("ctxT", [128, MC, T], F32, attn)
        first = ExitStack()
        em = sb("em", [128, KP, D + 2 * TP], F32, first)
        first.close()
        yb = sb("yb", [PAIR, 2, CG, YW], F32, attn)
        attn.close()

        xhi = sb("xhi", [128, MC, T], F32R)
        xlo = sb("xlo", [128, MC, T], F32R)
        cb = sb("cb", [128, RING, T])
        sg = sb("sg", [128, 2, TH])
        gu = sb("gu", [128, 2, TH])
        ac = sb("ac", [128, RING, TH])
        ahi = sb("ahi", [128, RING, TH], F32R)
        alo = sb("alo", [128, RING, TH], F32R)
        oT = sb("oT", [128, MC, T])
        cT = sb("cT", [E, T])
        NT = T // PAIR
        g_s = sb("g_s", [PAIR, NT, E])
        g_sc = sb("g_sc", [PAIR, NT, E])
        g_pair = sb("g_pair", [PAIR, NT * G, 6])
        g_gs = sb("g_gs", [PAIR, NT, G])
        g_gt = sb("g_gt", [PAIR, NT, G, G])
        g_eq = sb("g_eq", [PAIR, NT, G, G])
        g_rank = sb("g_rank", [PAIR, NT * G])
        g_gm = sb("g_gm", [PAIR, NT * G])
        g_mk = sb("g_mk", [PAIR, NT, E])
        g_top = sb("g_top", [PAIR, NT, TOPK])
        g_rep = sb("g_rep", [PAIR, NT, E])
        g_sel = sb("g_sel", [PAIR, NT, E])
        g_w = sb("g_w", [PAIR, NT, E])
        g_sum = sb("g_sum", [PAIR, NT])
        g_inv = sb("g_inv", [PAIR, NT])
        g_cw = sb("g_cw", [PAIR, NT, E])

        em_in = [sem(f"em_in{c}") for c in range(KP)]
        cst_in, wat_in, relv_in = sem("cst_in"), sem("wat_in"), sem("relv_in")
        wt_in = [sem(f"wt_in{s}") for s in range(RING)]
        cb_in = [sem(f"cb_in{s}") for s in range(RING)]
        z_out = [sem(f"z_out{g}") for g in range(NG)]
        z_in = [sem(f"z_in{g}") for g in range(NG)]
        y_out = [sem(f"y_out{g}") for g in range(NG)]
        y_in = [sem(f"y_in{g}") for g in range(NG)]
        comb_out, out_done = sem("comb_out"), sem("out_done")
        proj_done, h_ready = sem("proj_done"), sem("h_ready")
        mean_done, d_ready, sq_ready, var_done = sem("mean_done"), sem("d_ready"), sem("sq_ready"), sem("var_done")
        sd_ready, rs_ready, xn_ready = sem("sd_ready"), sem("rs_ready"), sem("xn_ready")
        qk_done, qk_copied = sem("qk_done"), sem("qk_copied")
        v_done, v_copied = sem("v_done"), sem("v_copied")
        shuf_ready, sin_ready, cos_ready = sem("shuf_ready"), sem("sin_ready"), sem("cos_ready")
        qrot_ready, krot_ready, qbd_ready = sem("qrot_ready"), sem("krot_ready"), sem("qbd_ready")
        ke_rel, zmask_ready, y_zero = sem("ke_rel"), sem("zmask_ready"), sem("y_zero")
        score_done, even_copied, odd_copied = sem("score_done"), sem("even_copied"), sem("odd_copied")
        sum_ready, max_ready, shift_ready = sem("sum_ready"), sem("max_ready"), sem("shift_ready")
        exp_ready, den_ready, inv_ready, prob_ready = sem("exp_ready"), sem("den_ready"), sem("inv_ready"), sem("prob_ready")
        tr_done, pt_even, pt_odd = sem("tr_done"), sem("pt_even"), sem("pt_odd")
        ctx_done, ctx_half, ctx_ready = sem("ctx_done"), sem("ctx_half"), sem("ctx_ready")
        wo_done, h2_ready = sem("wo_done"), sem("h2_ready")
        xhi_ready, xlo_ready = sem("xhi_ready"), sem("xlo_ready")
        logit_done, sig_ready, route, comb_ready = sem("logit_done"), sem("sig_ready"), sem("route"), sem("comb_ready")
        combT_done, combT_ready = sem("combT_done"), sem("combT_ready")
        ones_ready = sem("ones_ready")
        whi_ready, wlo_ready = sem("whi_ready"), sem("wlo_ready")
        gate_done, up_done, down_done = sem("gate_done"), sem("up_done"), sem("down_done")
        silu_ready, gu_ready, act_ready = sem("silu_ready"), sem("gu_ready"), sem("act_ready")
        ahi_ready, alo_ready, out_ready = sem("ahi_ready"), sem("alo_ready"), sem("out_ready")

        def half(t):
            return slice(t * TH, (t + 1) * TH)

        def col(a, n):
            return cs[:, a:a + n]

        ident = cs[:, C_ID:C_ID + 128]
        mean_w = cs[:, C_ONE:C_ONE + 128]
        hv = hT[:, :, :].rearrange("p m (b n) -> p m b n", n=L)

        def score_banks(st):
            return 4 * (st % 2)

        def skewed(dram, pitch, hh, g, q_step, start):
            row = NSTEP * CH * pitch
            return bass.AP(dram, hh * L * row + g * CG * pitch + start,
                           [[row + q_step, L], [pitch, CG], [1, L]])

        def copy_scores(eng, copy, st, copied):
            g, c = st // GRP, (st % GRP) * CH
            eng.wait_ge(score_done, st + 1)
            if g >= 2:
                eng.wait_ge(prob_ready, g - 1)
                eng.wait_ge(z_out[g - 2], 16)
            src = ps[0:PAIR, score_banks(st):score_banks(st) + 4, 0:IPS * PAIR].rearrange(
                "p j (i k) -> p j i k", k=PAIR)
            for dst, k in ((zb, L), (sc, 0)):
                copy(dst[:, g % 2, c:c + CH, 0:L].rearrange("p (j i) k -> p j i k", i=IPS),
                     src[:, :, :, k:k + L]).then_inc(copied, 1)

        def probs_trip(eng, g):
            eng.wait_ge(prob_ready, g + 1)
            eng.wait_ge(y_zero, 1)
            eng.dma_start(yd.ap()[:, g * CG:(g + 1) * CG, :], yb[:, g % 2, :, :]).then_inc(y_out[g], 16)
            eng.wait_ge(y_out[g], 16)
            for hh in range(2):
                eng.dma_start(yb[hh * L:(hh + 1) * L, g % 2, :, YW - L:YW],
                              skewed(yd, YW, hh, g, 1, 0)).then_inc(y_in[g], 16)

        block = ctx.enter_context(nc.Block())

        @block.sync
        def _(sp):
            for c in range(0, KP, 2):
                sp.dma_start(em[:, c, :], emb[c]).then_inc(em_in[c], 16)
            sp.dma_start(wat[:, :, :, :], wattn).then_inc(wat_in, 16)
            for n in range(RING):
                sp.dma_start(wst[:, n, :], wexp[n]).then_inc(wt_in[n], 16)
            for g in range(NG):
                sp.wait_ge(even_copied, 2 * (g + 1))
                sp.wait_ge(odd_copied, 2 * (g + 1))
                sp.wait_ge(zmask_ready, 1)
                sp.dma_start(zd.ap()[:, g * CG:(g + 1) * CG, :], zb[:, g % 2, :, :]).then_inc(z_out[g], 16)
                sp.wait_ge(z_out[g], 16)
                if g >= 2:
                    sp.wait_ge(sum_ready, g - 1)
                for hh in range(2):
                    sp.dma_start(rl[hh * L:(hh + 1) * L, g % 2, :, :],
                                 skewed(zd, ZW, hh, g, -1, L - 1)).then_inc(z_in[g], 16)
                if g >= 1:
                    probs_trip(sp, g - 1)
            probs_trip(sp, NG - 1)
            sp.wait_ge(combT_ready, 2)
            sp.dma_start(cd, cT[:, :]).then_inc(comb_out, 16)
            sp.wait_ge(comb_out, 16)

            def weights(n, slot):
                sp.wait_ge(whi_ready, n - RING + 1)
                sp.wait_ge(wlo_ready, n - RING + 1)
                sp.dma_start(wst[:, slot, :], wexp[n] if type(n) is int else
                             wexp[bass.ds(n, 1)].rearrange("o p w -> (o p) w")).then_inc(wt_in[slot], 16)

            def combine(n, slot):
                sp.wait_ge(act_ready, 2 * (n - RING) + 2)
                row = cd[n - NSH:n - NSH + 1, :] if type(n) is int else cd[bass.ds(n - NSH, 1), :]
                sp.dma_start(cb[:, slot, :], row.broadcast_to([128, T])).then_inc(cb_in[slot], 16)

            for n in range(NSH, RING):
                sp.dma_start(cb[:, n, :], cd[n - NSH:n - NSH + 1, :].broadcast_to([128, T])).then_inc(cb_in[n], 16)
            with sp.Fori(0, (NE - 2 - RING) // RING) as turn_of_ring:
                n0 = turn_of_ring * RING + (RING)
                for k in range(RING):
                    weights(n0 + k, k)
                    combine(n0 + k, k)
            for n in range(NE - 2, NE):
                weights(n, n % RING)
                combine(n, n % RING)
            sp.wait_ge(out_ready, 2 * MC)
            sp.dma_start(out.rearrange("m p t -> p m t"), oT[:, :, :]).then_inc(out_done, 16)
            sp.wait_ge(out_done, 16)

        @block.tensor
        def _(pe):
            for c in range(KP):
                pe.wait_ge(em_in[c], 16)
                for t in range(2):
                    for m in range(MC):
                        mm = nc.tensor.matmul(ps[:, 2 * t + m, 0:TP], em[:, c, m * 128:(m + 1) * 128],
                                              em[:, c, D + t * TP:D + (t + 1) * TP],
                                              start=(c == 0), stop=(c == KP - 1))
                        if c == KP - 1:
                            mm.then_inc(proj_done, 1)

            def norm_stats(k):
                for t in range(2):
                    if k == 0:
                        pe.wait_ge(h_ready, MC + MC * (t + 1))
                    else:
                        pe.wait_ge(h2_ready, MC * (t + 1))
                    for m in range(MC):
                        mm = nc.tensor.matmul(ps[:, 4 + t, 0:TH], mean_w, hT[:, m, half(t)],
                                              start=(m == 0), stop=(m == MC - 1))
                    mm.then_inc(mean_done, 1)
                for t in range(2):
                    pe.wait_ge(sq_ready, 2 * k + t + 1)
                    for m in range(MC):
                        mm = nc.tensor.matmul(ps[:, 6 + t, 0:TH], mean_w, sq[:, m, half(t)],
                                              start=(m == 0), stop=(m == MC - 1))
                    mm.then_inc(var_done, 1)

            pe.wait_ge(cst_in, 16)
            norm_stats(0)

            pe.wait_ge(wat_in, 16)
            for t in range(2):
                pe.wait_ge(xn_ready, t + 1)
                for mat in range(2):
                    for s in range(MC):
                        for m in range(MC):
                            mm = nc.tensor.matmul(ps[:, 4 * t + 2 * mat + s, 0:TH],
                                                  wat[:, mat, m, s * 128:(s + 1) * 128], xn[:, m, half(t)],
                                                  start=(m == 0), stop=(m == MC - 1))
                        mm.then_inc(qk_done, 1)
            for i in range(B // 2):
                pe.wait_ge(qk_copied, i + 1)
                for j in range(2):
                    b = 2 * i + j
                    for m in range(MC):
                        mm = nc.tensor.matmul(ps[0:L, i, j * D:(j + 1) * D], xn[:, m, b * L:(b + 1) * L],
                                              wat[:, 2, m, :], start=(m == 0), stop=(m == MC - 1))
                mm.then_inc(v_done, 1)
            for st in range(NSTEP):
                s = st // (NSTEP // MC)
                if st == 0:
                    pe.wait_ge(v_copied, B // 2)
                    pe.wait_ge(ke_rel, MC)
                if st % (NSTEP // MC) == 0:
                    pe.wait_ge(krot_ready, s + 1)
                    pe.wait_ge(qbd_ready, 2 * (s + 1))
                if st >= 2:
                    pe.wait_ge(odd_copied if st % 2 else even_copied, 2 * (st // 2))
                for i in range(IPS):
                    b = IPS * (st % (B // IPS)) + i
                    for j in range(4):
                        mm = nc.tensor.matmul(ps[0:PAIR, score_banks(st) + j, i * PAIR:(i + 1) * PAIR],
                                              qbd[32 * j:32 * j + 32, s, b, :], ke[32 * j:32 * j + 32, s, b, :],
                                              start=True, stop=True)
                mm.then_inc(score_done, 1)

            def turn(u):
                st = u // 2
                if u % (2 * GRP) == 0:
                    pe.wait_ge(y_in[st // GRP], 32)
                if u == 0:
                    pe.wait_ge(even_copied, NSTEP)
                    pe.wait_ge(odd_copied, NSTEP)
                if u >= 2:
                    pe.wait_ge(pt_odd if u % 2 else pt_even, u // 2)
                for k in range(CH // 2):
                    c = (st % GRP) * CH + (u % 2) * (CH // 2) + k
                    mm = nc.tensor.transpose(ps[0:PAIR, 2 * (u % 2) + k // 4, (k % 4) * PAIR:(k % 4 + 1) * PAIR],
                                             yb[:, (st // GRP) % 2, c, L - 1:YW], ident[0:PAIR, 0:PAIR])
                mm.then_inc(tr_done, 1)

            def context(st):
                s = st // (NSTEP // MC)
                pe.wait_ge(pt_even, st + 1)
                pe.wait_ge(pt_odd, st + 1)
                if st == 0:
                    pe.wait_ge(relv_in, 16)
                if st >= 4:
                    pe.wait_ge(ctx_ready, st - 3)
                for i in range(IPS):
                    b = IPS * (st % (B // IPS)) + i
                    for j in range(4):
                        k = 4 * j + i
                        mm = nc.tensor.matmul(ps[32 * j:32 * j + 32, 4 + st % 4, i * PAIR:(i + 1) * PAIR],
                                              ve[:, b, s * 128 + 32 * j:s * 128 + 32 * j + 32],
                                              pt[:, (2 * st + k // 8) % 4, k % 8, :], start=True, stop=True)
                mm.then_inc(ctx_done, 1)

            for st in range(NSTEP):
                turn(2 * st)
                turn(2 * st + 1)
                if st >= 1:
                    context(st - 1)
            context(NSTEP - 1)
            for t in range(2):
                pe.wait_ge(ctx_ready, NSTEP)
                for m in range(MC):
                    for s in range(MC):
                        mm = nc.tensor.matmul(ps[:, 2 * t + m, 0:TH], wat[:, 3, s, m * 128:(m + 1) * 128],
                                              ctxT[:, s, half(t)], start=(s == 0), stop=(s == MC - 1))
                    mm.then_inc(wo_done, 1)
            norm_stats(1)
            pe.wait_ge(xn_ready, 4)
            for i in range(NT):
                for m in range(MC):
                    mm = nc.tensor.matmul(ps[0:PAIR, 0, i * E:(i + 1) * E], xn[:, m, i * PAIR:(i + 1) * PAIR],
                                          cs[:, C_GW + m * E:C_GW + (m + 1) * E],
                                          start=(m == 0), stop=(m == MC - 1))
            mm.then_inc(logit_done, 1)

            def gate_up(n, slot, t, waits_pair):
                u = 2 * n + t
                if t == 0:
                    pe.wait_ge(whi_ready, n + 1)
                    pe.wait_ge(wlo_ready, n + 1)
                if waits_pair:
                    pe.wait_ge(gu_ready, u - 1)
                for mat, done in ((0, gate_done), (1, up_done)):
                    o = ps[:, 2 * t + mat, 0:TH]
                    k = 0
                    for m in range(MC):
                        a = (2 * mat + m) * 128
                        for w, x in ((whi, xhi), (whi, xlo), (wlo, xhi)):
                            mm = nc.tensor.matmul(o, w[:, slot, a:a + 128], x[:, m, half(t)],
                                                  start=(k == 0), stop=(k == 3 * MC - 1))
                            k += 1
                    mm.then_inc(done, 1)

            def down(n, slot, t, start, stop):
                u = 2 * n + t
                pe.wait_ge(ahi_ready, u + 1)
                pe.wait_ge(alo_ready, u + 1)
                r = (2 * slot + t) % RING
                for m in range(MC):
                    a = (4 + m) * 128
                    for k, (w, x) in enumerate(((whi, ahi), (whi, alo), (wlo, ahi))):
                        mm = nc.tensor.matmul(ps[:, 4 + 2 * t + m, 0:TH], w[:, slot, a:a + 128], x[:, r, :],
                                              start=(start and k == 0), stop=(stop and k == 2),
                                              skip_group_check=True)
                mm.then_inc(down_done, 1)

            pe.wait_ge(xhi_ready, 2)
            pe.wait_ge(xlo_ready, 2)
            pe.wait_ge(sig_ready, 1)
            gate_up(0, 0, 0, False)
            gate_up(0, 0, 1, False)
            gate_up(1, 1, 0, True)
            down(0, 0, 0, True, False)
            gate_up(1, 1, 1, True)
            down(0, 0, 1, True, False)
            pe.wait_ge(comb_ready, 1)
            pe.wait_ge(gu_ready, 3)
            for i in range(NT):
                mm = nc.tensor.transpose(ps[0:E, i // 4, (i % 4) * PAIR:(i % 4 + 1) * PAIR], g_cw[:, i, :],
                                         ident[0:PAIR, 0:PAIR])
            mm.then_inc(combT_done, 1)
            pe.wait_ge(combT_ready, 2)

            def expert(n, slot):
                gate_up(n, slot, 0, True)
                down(n - 1, (slot - 1) % RING, 0, False, False)
                gate_up(n, slot, 1, True)
                down(n - 1, (slot - 1) % RING, 1, False, False)

            with pe.Fori(0, (NE - NSH) // RING) as turn_of_ring:
                n0 = turn_of_ring * RING + (NSH)
                for k in range(RING):
                    expert(n0 + k, (NSH + k) % RING)
            down(NE - 1, (NE - 1) % RING, 0, False, True)
            down(NE - 1, (NE - 1) % RING, 1, False, True)

        @block.vector
        def _(dve):
            dve.wait_ge(cst_in, 16)
            for m in range(MC):
                nc.vector.tensor_tensor(hv[:, m, :, 0], col(C_CLS + m, 1).broadcast_to([128, B]),
                                        col(C_POS + m * L, 1).broadcast_to([128, B]), ALU.add).then_inc(h_ready, 1)
            for t in range(2):
                for m in range(MC):
                    dve.wait_ge(proj_done, 2 * t + m + 1)
                    nc.vector.scalar_tensor_tensor(
                        out=hv[:, m, t * HB:(t + 1) * HB, 1:L],
                        in0=ps[:, 2 * t + m, 0:TP].rearrange("p (b n) -> p b n", n=NP),
                        scalar=col(C_BIAS + m, 1),
                        in1=cs[:, C_POS + m * L + 1:C_POS + (m + 1) * L].unsqueeze(1).broadcast_to([128, HB, NP]),
                        op0=ALU.add, op1=ALU.add).then_inc(h_ready, 1)

            def norm(k):
                for t in range(2):
                    dve.wait_ge(mean_done, 2 * k + t + 1)
                    nc.vector.tensor_tensor(dT[:, :, half(t)], hT[:, :, half(t)],
                                            ps[:, 4 + t, 0:TH].unsqueeze(1).broadcast_to([128, MC, TH]),
                                            ALU.subtract).then_inc(d_ready, 1)
                for t in range(2):
                    dve.wait_ge(sd_ready, 2 * k + t + 1)
                    nc.vector.reciprocal(rs[:, half(t)], sd[:, half(t)]).then_inc(rs_ready, 1)
                    dve.wait_ge(rs_ready, 2 * k + t + 1)
                    nc.vector.tensor_tensor(xn[:, :, half(t)], dT[:, :, half(t)],
                                            rs[:, half(t)].unsqueeze(1).broadcast_to([128, MC, TH]),
                                            ALU.mult).then_inc(xn_ready, 1)

            norm(0)

            swap = [i ^ 1 for i in range(32)]
            for s in range(MC):
                dve.wait_ge(qk_copied, 8)
                if s:
                    dve.wait_ge(krot_ready, s)
                nc.vector.stream_shuffle(qksw[:, :, :], qk[:, :, s, :], swap).then_inc(shuf_ready, 1)
                dve.wait_ge(shuf_ready, s + 1)
                v = qksw[:, :, :].rearrange("p a (b n) -> p (a b) n", n=L)
                nc.vector.tensor_tensor(v, v, col(C_SIN, L).unsqueeze(1).broadcast_to([128, 2 * B, L]),
                                        ALU.mult).then_inc(sin_ready, 1)
                dve.wait_ge(sin_ready, s + 1)
                dve.wait_ge(cos_ready, s + 1)
                nc.vector.tensor_tensor(qrot[:, s, :], qksw[:, 0, :], qkc[:, 0, :], ALU.add).then_inc(qrot_ready, 1)
                nc.vector.tensor_tensor(ke[:, s, :, 0:L], qksw[:, 1, :].rearrange("p (b n) -> p b n", n=L),
                                        qkc[:, 1, :].rearrange("p (b n) -> p b n", n=L),
                                        ALU.add).then_inc(krot_ready, 1)

            def softmax_top(g):
                x = sc[:, g % 2, :, :]
                dve.wait_ge(z_in[g], 32)
                dve.wait_ge(even_copied, 2 * (g + 1))
                dve.wait_ge(odd_copied, 2 * (g + 1))
                nc.vector.tensor_tensor(x, x, rl[:, g % 2, :, :], ALU.add).then_inc(sum_ready, 1)
                dve.wait_ge(sum_ready, g + 1)
                nc.vector.tensor_reduce(st_mx[:, :], x, AX_X, ALU.max).then_inc(max_ready, 1)
                dve.wait_ge(max_ready, g + 1)
                nc.vector.tensor_tensor(x, x, st_mx[:, :].unsqueeze(2).broadcast_to([PAIR, CG, L]),
                                        ALU.subtract).then_inc(shift_ready, 1)

            def softmax_bottom(g):
                x = sc[:, g % 2, :, :]
                dve.wait_ge(exp_ready, g + 1)
                nc.vector.tensor_reduce(st_sum[:, :], x, AX_X, ALU.add).then_inc(den_ready, 1)
                dve.wait_ge(den_ready, g + 1)
                nc.vector.reciprocal(st_inv[:, :], st_sum[:, :]).then_inc(inv_ready, 1)
                dve.wait_ge(inv_ready, g + 1)
                if g == 0:
                    dve.wait_ge(y_zero, 1)
                if g >= 2:
                    dve.wait_ge(tr_done, 2 * GRP * (g - 1))
                nc.vector.tensor_tensor(yb[:, g % 2, :, L - 1:2 * L - 1], x,
                                        st_inv[:, :].unsqueeze(2).broadcast_to([PAIR, CG, L]),
                                        ALU.mult).then_inc(prob_ready, 1)

            def turn_copy(st):
                dve.wait_ge(tr_done, 2 * st + 2)
                if st >= 2:
                    dve.wait_ge(ctx_done, st - 1)
                nc.vector.tensor_copy(pt[:, (2 * st + 1) % 4, :, :].rearrange("p (a k) c -> p a (k c)", a=2),
                                      ps[0:PAIR, 2:4, 0:4 * PAIR]).then_inc(pt_odd, 1)

            def context_add(st):
                dve.wait_ge(ctx_done, st + 1)
                dve.wait_ge(ctx_half, st + 1)
                b0 = IPS * (st % (B // IPS))
                nc.vector.scalar_tensor_tensor(
                    out=ctxT[:, st // (NSTEP // MC), b0 * L:(b0 + IPS) * L].rearrange("p (i q) -> p i q", q=L),
                    in0=ps[:, 4 + st % 4, 0:IPS * PAIR].rearrange("p (i k) -> p i k", k=PAIR)[:, :, L:PAIR],
                    scalar=col(C_OM + 1, 1), in1=cth[:, st % 2, :, :],
                    op0=ALU.mult, op1=ALU.add).then_inc(ctx_ready, 1)

            for st in range(1, GRP * 2, 2):
                copy_scores(dve, nc.vector.tensor_copy, st, odd_copied)
            softmax_top(0)
            for g in range(NG):
                if g >= 2:
                    for st in range(GRP * (g - 2), GRP * (g - 1)):
                        turn_copy(st)
                        if st >= 1:
                            context_add(st - 1)
                softmax_bottom(g)
                if g + 2 < NG:
                    copy_scores(dve, nc.vector.tensor_copy, GRP * (g + 2) + 1, odd_copied)
                if g + 1 < NG:
                    softmax_top(g + 1)
            for st in range(GRP * (NG - 2), NSTEP):
                turn_copy(st)
                if st >= 1:
                    context_add(st - 1)
            context_add(NSTEP - 1)

            for t in range(2):
                for m in range(MC):
                    dve.wait_ge(wo_done, 2 * t + m + 1)
                    nc.vector.tensor_tensor(hT[:, m, half(t)], hT[:, m, half(t)], ps[:, 2 * t + m, 0:TH],
                                            ALU.add).then_inc(h2_ready, 1)
            norm(1)
            for t in range(2):
                dve.wait_ge(xhi_ready, t + 1)
                nc.vector.tensor_tensor(xlo[:, :, half(t)], xn[:, :, half(t)],
                                        xhi[:, :, half(t)].bitcast(F32), ALU.subtract).then_inc(xlo_ready, 1)

            def split_low(n, slot, waits_slot):
                dve.wait_ge(whi_ready, n + 1)
                if waits_slot:
                    dve.wait_ge(down_done, 2 * (n - RING) + 2)
                nc.vector.tensor_tensor(wlo[:, slot, :], wst[:, slot, :], whi[:, slot, :].bitcast(F32),
                                        ALU.subtract).then_inc(wlo_ready, 1)

            def gate_times_up(n, t, waits_ring):
                u = 2 * n + t
                dve.wait_ge(silu_ready, u + 1)
                dve.wait_ge(up_done, u + 1)
                if waits_ring:
                    dve.wait_ge(act_ready, u - 1)
                nc.vector.tensor_tensor(gu[:, t, :], sg[:, t, :], ps[:, 2 * t + 1, 0:TH],
                                        ALU.mult).then_inc(gu_ready, 1)

            def act_low(n, slot, t, waits_ring):
                u = 2 * n + t
                r = (2 * slot + t) % RING
                dve.wait_ge(ahi_ready, u + 1)
                if waits_ring:
                    dve.wait_ge(down_done, u - RING + 1)
                nc.vector.tensor_tensor(alo[:, r, :], ac[:, r, :], ahi[:, r, :].bitcast(F32),
                                        ALU.subtract).then_inc(alo_ready, 1)

            count = [0]

            def routed(ins):
                count[0] += 1
                ins.then_inc(route, 1)
                dve.wait_ge(route, count[0])

            def route_groups():
                dve.wait_ge(sig_ready, 1)
                routed(nc.vector.tensor_tensor(g_sc[:, :, :], g_s[:, :, :],
                                               cs[0:PAIR, C_GB:C_GB + E].unsqueeze(1).broadcast_to([PAIR, NT, E]),
                                               ALU.add))
                q = g_sc[:, :, :].rearrange("p t (g e) -> p (t g) e", e=GE)
                nc.vector.tensor_tensor(g_pair[:, :, 0:3], q[:, :, 0:3], q[:, :, 1:4], ALU.add)
                nc.vector.tensor_tensor(g_pair[:, :, 3:5], q[:, :, 0:2], q[:, :, 2:4], ALU.add)
                routed(nc.vector.tensor_tensor(g_pair[:, :, 5:6], q[:, :, 0:1], q[:, :, 3:4], ALU.add))
                routed(nc.vector.tensor_reduce(g_gs[:, :, :].rearrange("p t g -> p (t g)"), g_pair[:, :, :],
                                               AX_X, ALU.max))

            def route_masked():
                mine = g_gs[:, :, :].unsqueeze(3).broadcast_to([PAIR, NT, G, G])
                other = g_gs[:, :, :].unsqueeze(2).broadcast_to([PAIR, NT, G, G])
                low = cs[0:PAIR, C_LOW:C_LOW + G * G].rearrange("p (g h) -> p g h", h=G)
                nc.vector.tensor_tensor(g_gt[:, :, :, :], other, mine, ALU.is_gt)
                routed(nc.vector.tensor_tensor(g_eq[:, :, :, :], other, mine, ALU.is_equal))
                routed(nc.vector.tensor_tensor(g_eq[:, :, :, :], g_eq[:, :, :, :],
                                               low.unsqueeze(1).broadcast_to([PAIR, NT, G, G]), ALU.mult))
                routed(nc.vector.tensor_tensor(g_gt[:, :, :, :], g_gt[:, :, :, :], g_eq[:, :, :, :], ALU.add))
                routed(nc.vector.tensor_reduce(g_rank[:, :], g_gt[:, :, :, :].rearrange("p t g h -> p (t g) h"),
                                               AX_X, ALU.add))
                routed(nc.vector.tensor_scalar(g_gm[:, :], g_rank[:, :], TKG - 0.5, None, ALU.is_lt))
                routed(nc.vector.tensor_tensor(g_mk[:, :, :].rearrange("p t (g e) -> p (t g) e", e=GE),
                                               g_sc[:, :, :].rearrange("p t (g e) -> p (t g) e", e=GE),
                                               g_gm[:, :].unsqueeze(2).broadcast_to([PAIR, NT * G, GE]), ALU.mult))

            def route_top():
                for i in range(NT):
                    ins = nc.vector.max(g_top[:, i, :], g_mk[:, i, :])
                routed(ins)
                for i in range(NT):
                    ins = nc.vector.match_replace(g_rep[:, i, :], g_top[:, i, :], g_mk[:, i, :], -3e38)
                routed(ins)

            def route_weights():
                routed(nc.vector.tensor_tensor(g_sel[:, :, :], g_rep[:, :, :], g_mk[:, :, :], ALU.not_equal))
                routed(nc.vector.tensor_tensor(g_w[:, :, :], g_s[:, :, :], g_sel[:, :, :], ALU.mult))
                routed(nc.vector.tensor_reduce(g_sum[:, :], g_w[:, :, :], AX_X, ALU.add))
                routed(nc.vector.tensor_scalar(g_sum[:, :], g_sum[:, :], 1e-20, None, ALU.add))
                routed(nc.vector.reciprocal(g_inv[:, :], g_sum[:, :]))
                routed(nc.vector.tensor_scalar(g_inv[:, :], g_inv[:, :], SCALE, None, ALU.mult))
                nc.vector.tensor_tensor(g_cw[:, :, :], g_w[:, :, :],
                                        g_inv[:, :].unsqueeze(2).broadcast_to([PAIR, NT, E]),
                                        ALU.mult).then_inc(comb_ready, 1)

            for n in range(NSH + 1):
                split_low(n, n, False)
            route_groups()
            gate_times_up(0, 0, False)
            route_masked()
            gate_times_up(0, 1, False)
            act_low(0, 0, 0, False)
            route_top()
            gate_times_up(1, 0, True)
            act_low(0, 0, 1, False)
            route_weights()
            gate_times_up(1, 1, True)
            act_low(1, 1, 0, False)

            def expert(n, slot, last, waits_slot=True):
                if not last:
                    split_low(n + 1, (slot + 1) % RING, waits_slot)
                gate_times_up(n, 0, True)
                act_low(n - 1, (slot - 1) % RING, 1, True)
                gate_times_up(n, 1, True)
                act_low(n, slot, 0, True)

            split_low(NSH + 1, NSH + 1, False)
            gate_times_up(NSH, 0, True)
            act_low(NSH - 1, NSH - 1, 1, False)
            gate_times_up(NSH, 1, True)
            act_low(NSH, NSH, 0, True)
            with dve.Fori(0, (NE - 3 - NSH + 1) // RING) as turn_of_ring:
                n0 = turn_of_ring * RING + (NSH + 1)
                for k in range(RING):
                    expert(n0 + k, (NSH + 1 + k) % RING, False)
            for n in range(NE - 3, NE):
                expert(n, n % RING, n == NE - 1)
            act_low(NE - 1, (NE - 1) % RING, 1, True)
            for t in range(2):
                for m in range(MC):
                    dve.wait_ge(down_done, 2 * NE - 1 + t)
                    nc.vector.tensor_tensor(oT[:, m, half(t)], hT[:, m, half(t)], ps[:, 4 + 2 * t + m, 0:TH],
                                            ALU.add).then_inc(out_ready, 1)

        @block.scalar
        def _(act):
            act.dma_start(cs[:, :], cst).then_inc(cst_in, 16)
            for c in range(1, KP, 2):
                act.dma_start(em[:, c, :], emb[c]).then_inc(em_in[c], 16)
            act.dma_start(ve[L:PAIR, :, :], rel_v.unsqueeze(1).broadcast_to([L, B, D])).then_inc(relv_in, 16)

            def norm(k):
                for t in range(2):
                    act.wait_ge(d_ready, 2 * k + t + 1)
                    nc.scalar.activation(sq[:, :, half(t)], dT[:, :, half(t)], ACT.Square).then_inc(sq_ready, 1)
                for t in range(2):
                    act.wait_ge(var_done, 2 * k + t + 1)
                    nc.scalar.activation(sd[:, half(t)], ps[:, 6 + t, 0:TH], ACT.Sqrt,
                                         bias=col(C_EPS, 1)).then_inc(sd_ready, 1)

            act.wait_ge(cst_in, 16)
            norm(0)
            for t in range(2):
                for mat in range(2):
                    for s in range(MC):
                        i = 4 * t + 2 * mat + s
                        act.wait_ge(qk_done, i + 1)
                        nc.scalar.copy(qk[:, mat, s, half(t)], ps[:, i, 0:TH]).then_inc(qk_copied, 1)
            for i in range(B // 2):
                act.wait_ge(v_done, i + 1)
                nc.scalar.copy(ve[0:L, 2 * i:2 * i + 2, :].rearrange("p b d -> p (b d)"),
                               ps[0:L, i, :]).then_inc(v_copied, 1)

            def block_diagonal(s):
                act.wait_ge(qrot_ready, s + 1)
                for hh in range(2):
                    nc.scalar.activation(qbd[:, s, :, hh * L:(hh + 1) * L],
                                         qrot[:, s, :].rearrange("p (b n) -> p b n", n=L), ACT.Copy,
                                         scale=col(C_QM + hh, 1)).then_inc(qbd_ready, 1)

            def exponent(g):
                act.wait_ge(shift_ready, g + 1)
                nc.scalar.activation(sc[:, g % 2, :, :], sc[:, g % 2, :, :], ACT.Exp).then_inc(exp_ready, 1)

            def turn_copy(st):
                act.wait_ge(tr_done, 2 * st + 1)
                if st >= 2:
                    act.wait_ge(ctx_done, st - 1)
                nc.scalar.copy(pt[:, (2 * st) % 4, :, :].rearrange("p (a k) c -> p a (k c)", a=2),
                               ps[0:PAIR, 0:2, 0:4 * PAIR]).then_inc(pt_even, 1)

            def context_half(st):
                act.wait_ge(ctx_done, st + 1)
                if st >= 2:
                    act.wait_ge(ctx_ready, st - 1)
                nc.scalar.activation(cth[:, st % 2, :, :],
                                     ps[:, 4 + st % 4, 0:IPS * PAIR].rearrange(
                                         "p (i k) -> p i k", k=PAIR)[:, :, 0:L],
                                     ACT.Copy, scale=col(C_OM, 1)).then_inc(ctx_half, 1)

            block_diagonal(0)
            block_diagonal(1)
            for st in range(0, GRP * 2, 2):
                copy_scores(act, nc.scalar.copy, st, even_copied)
            exponent(0)
            for g in range(NG):
                if g >= 2:
                    for st in range(GRP * (g - 2), GRP * (g - 1)):
                        turn_copy(st)
                        if st >= 1:
                            context_half(st - 1)
                if g + 2 < NG:
                    copy_scores(act, nc.scalar.copy, GRP * (g + 2), even_copied)
                if g + 1 < NG:
                    exponent(g + 1)
            for st in range(GRP * (NG - 2), NSTEP):
                turn_copy(st)
                if st >= 1:
                    context_half(st - 1)
            context_half(NSTEP - 1)

            norm(1)
            for t in range(2):
                act.wait_ge(xn_ready, 2 + t + 1)
                nc.scalar.copy(xhi[:, :, half(t)], xn[:, :, half(t)]).then_inc(xhi_ready, 1)

            def split_high(n, slot, waits_slot):
                if type(n) is int:
                    act.wait_ge(wt_in[slot], 16 * (n // RING + 1))
                else:
                    act.wait_ge(wt_in[slot], 4 * (n - slot) + 16)
                if waits_slot:
                    act.wait_ge(down_done, 2 * (n - RING) + 2)
                nc.scalar.copy(whi[:, slot, :], wst[:, slot, :]).then_inc(whi_ready, 1)

            def silu(n, t, waits_ring):
                u = 2 * n + t
                act.wait_ge(gate_done, u + 1)
                if waits_ring:
                    act.wait_ge(gu_ready, u - 1)
                nc.scalar.activation(sg[:, t, :], ps[:, 2 * t, 0:TH], ACT.Silu).then_inc(silu_ready, 1)

            def act_high(n, slot, t, waits_ring):
                u = 2 * n + t
                r = (2 * slot + t) % RING
                act.wait_ge(act_ready, u + 1)
                if waits_ring:
                    act.wait_ge(down_done, u - RING + 1)
                nc.scalar.copy(ahi[:, r, :], ac[:, r, :]).then_inc(ahi_ready, 1)

            for n in range(NSH + 1):
                split_high(n, n, False)
            act.wait_ge(logit_done, 1)
            nc.scalar.activation(g_s[:, :, :].rearrange("p t e -> p (t e)"), ps[0:PAIR, 0, 0:NT * E],
                                 ACT.Sigmoid).then_inc(sig_ready, 1)
            silu(0, 0, False)
            silu(0, 1, False)
            act_high(0, 0, 0, False)
            silu(1, 0, True)
            act_high(0, 0, 1, False)
            silu(1, 1, True)
            act_high(1, 1, 0, False)
            act_high(1, 1, 1, False)
            act.wait_ge(combT_done, 1)
            for i in range(2):
                nc.scalar.copy(cT[:, half(i)], ps[0:E, i, 0:TH]).then_inc(combT_ready, 1)

            def expert(n, slot, last, waits_slot=True):
                if not last:
                    split_high(n + 1, (slot + 1) % RING, waits_slot)
                silu(n, 0, True)
                act_high(n - 1, (slot - 1) % RING, 1, True)
                silu(n, 1, True)
                act_high(n, slot, 0, True)

            split_high(NSH + 1, NSH + 1, False)
            silu(NSH, 0, True)
            silu(NSH, 1, True)
            act_high(NSH, NSH, 0, True)
            with act.Fori(0, (NE - 3 - NSH + 1) // RING) as turn_of_ring:
                n0 = turn_of_ring * RING + (NSH + 1)
                for k in range(RING):
                    expert(n0 + k, (NSH + 1 + k) % RING, False)
            for n in range(NE - 3, NE):
                expert(n, n % RING, n == NE - 1)
            act_high(NE - 1, (NE - 1) % RING, 1, True)

        @block.gpsimd
        def _(pool):
            nc.gpsimd.memset(zb[:, :, :, L:ZW], NEG).then_inc(zmask_ready, 1)
            pool.wait_ge(cst_in, 16)
            for s in range(MC):
                nc.gpsimd.tensor_copy(ke[:, s, :, L:PAIR],
                                      col(C_REL, L).unsqueeze(1).broadcast_to([128, B, L])).then_inc(ke_rel, 1)
            pool.wait_ge(proj_done, 2 * MC)
            nc.gpsimd.memset(yb[:, :, :, :], 0.0).then_inc(y_zero, 1)
            for s in range(MC):
                pool.wait_ge(qk_copied, 8)
                if s:
                    pool.wait_ge(krot_ready, s)
                nc.gpsimd.tensor_tensor(
                    qkc[:, :, :].rearrange("p a (b n) -> p a b n", n=L),
                    qk[:, :, s, :].rearrange("p a (b n) -> p a b n", n=L),
                    col(C_COS, L).unsqueeze(1).unsqueeze(1).broadcast_to([128, 2, B, L]),
                    ALU.mult).then_inc(cos_ready, 1)

            pool.wait_ge(wo_done, 2 * MC)
            for n in range(NSH):
                nc.gpsimd.memset(cb[:, n, :], 1.0).then_inc(ones_ready, 1)
            pool.wait_ge(ones_ready, NSH)

            def weigh(n, slot, t, waits_ring):
                u = 2 * n + t
                r = (2 * slot + t) % RING
                pool.wait_ge(gu_ready, u + 1)
                if waits_ring:
                    pool.wait_ge(ahi_ready, u - RING + 1)
                    pool.wait_ge(alo_ready, u - RING + 1)
                nc.gpsimd.tensor_tensor(ac[:, r, :], gu[:, t, :], cb[:, slot, half(t)],
                                        ALU.mult).then_inc(act_ready, 1)

            for n in range(NSH):
                weigh(n, n, 0, False)
                weigh(n, n, 1, False)
            for n in range(NSH, RING):
                pool.wait_ge(cb_in[n], 16)
                weigh(n, n, 0, True)
                weigh(n, n, 1, True)
            with pool.Fori(0, (NE - 2 - RING) // RING) as turn_of_ring:
                n0 = turn_of_ring * RING + (RING)
                for k in range(RING):
                    pool.wait_ge(cb_in[k], 4 * n0 if k < NSH else 4 * n0 + 16)
                    weigh(n0 + k, k, 0, True)
                    weigh(n0 + k, k, 1, True)
            for n in range(NE - 2, NE):
                pool.wait_ge(cb_in[n % RING], 16 * (n // RING))
                weigh(n, n % RING, 0, True)
                weigh(n, n % RING, 1, True)


def tables():
    inv = (1.0 / np.float32(10000.0) ** (np.arange(0, HD, 2, dtype=np.float32) / np.float32(HD))).astype(np.float32)
    ang = np.outer(np.arange(L, dtype=np.float32), inv).astype(np.float32)
    f = (np.arange(128) % HD) // 2
    cos = np.cos(ang)[:, f].T.astype(np.float32)
    sin = np.sin(ang)[:, f].T.astype(np.float32)
    sin = np.where((np.arange(128) % 2 == 0)[:, None], -sin, sin)
    first = (np.arange(128) % 32 < HD).astype(np.float32)
    pair = np.stack([first, 1 - first], 1)
    low = np.broadcast_to((np.arange(G)[None, :] < np.arange(G)[:, None]).astype(np.float32).reshape(1, G * G),
                          (128, G * G))
    return cos, sin, pair, low


def kernel(x, L0_tok_W, L0_tok_b, L0_tok_class_token, L0_tok_pos_embedding, L0_attn_w_q, L0_attn_w_k, L0_attn_w_v,
           L0_attn_w_o, L0_attn_rel_emb, L0_ffn_gate_w, L0_ffn_gate_bias, L0_ffn_w_gate, L0_ffn_w_up, L0_ffn_w_down,
           L0_ffn_sh_gate, L0_ffn_sh_up, L0_ffn_sh_down):
    import concourse.bacc as bacc
    from concourse.bass_utils import run_bass_kernel_spmd

    a = np.asarray
    P = 16
    pat = a(x).reshape(B, 3, 6, P, 6, P).transpose(1, 3, 5, 0, 2, 4).reshape(KP, 128, B * NP)
    wtok = a(L0_tok_W).T.reshape(KP, 128, D)
    emb = np.ascontiguousarray(np.concatenate([wtok, pat], axis=2))
    offs = np.clip(np.arange(L) - (L - 1), -32, 32) + 32
    rel = a(L0_attn_rel_emb)[offs]
    rel_v = np.ascontiguousarray(np.tile(rel, (1, D // HD)))
    cos, sin, pair, low = tables()

    def cols(v):
        return v.reshape(-1, MC, 128).transpose(2, 1, 0).reshape(128, -1)

    const = np.ascontiguousarray(np.concatenate([
        cols(a(L0_tok_b)), cols(a(L0_tok_class_token)), cols(a(L0_tok_pos_embedding)[0]), cos, sin,
        pair * np.float32(0.25), pair, np.tile(rel.T, (128 // HD, 1)), cols(a(L0_ffn_gate_w)),
        np.broadcast_to(a(L0_ffn_gate_bias), (128, E)), low, np.full((128, 1), EPS), np.full((128, 128), 1 / D),
        np.eye(128)], axis=1), dtype=np.float32)
    wattn = np.ascontiguousarray(np.stack([a(w).T.reshape(MC, 128, D).transpose(1, 0, 2) for w in
                                           (L0_attn_w_q, L0_attn_w_k, L0_attn_w_v, L0_attn_w_o)], axis=1))

    def side(w):
        return w.reshape(-1, INTER, MC, 128).transpose(0, 3, 2, 1).reshape(-1, 128, D)

    wexp = np.ascontiguousarray(np.concatenate([
        np.concatenate([side(a(L0_ffn_sh_gate)), side(a(L0_ffn_w_gate))]),
        np.concatenate([side(a(L0_ffn_sh_up)), side(a(L0_ffn_w_up))]),
        np.concatenate([a(L0_ffn_sh_down).reshape(D, NSH, INTER).transpose(1, 2, 0),
                        a(L0_ffn_w_down).transpose(0, 2, 1)])], axis=2))

    nc = bacc.Bacc("TRN2", target_bir_lowering=False, num_devices=1)
    arrays = {"emb": emb, "cst": const, "rel_v": rel_v, "wattn": wattn, "wexp": wexp}
    aps = [nc.dram_tensor(n, v.shape, F32, kind="ExternalInput").ap() for n, v in arrays.items()]
    aps.append(nc.dram_tensor("out", (MC, 128, T), F32, kind="ExternalOutput").ap())
    build(nc, *aps)
    r = run_bass_kernel_spmd(nc, [arrays], core_ids=[0])
    return np.ascontiguousarray(r.results[0]["out"].reshape(MC, 128, B, L).transpose(2, 3, 0, 1).reshape(B, L, D))
```

```python
from contextlib import ExitStack

import numpy as np

import concourse.bass as bass
from concourse import mybir

F32 = mybir.dt.float32
F32R = mybir.dt.float32r
ALU = mybir.AluOpType
ACT = mybir.ActivationFunctionType
AX_X = mybir.AxisListType.X

B, L, D = 16, 37, 256
NP = L - 1
T = B * L
KP = 768 // 128
MC = D // 128
HB = B // 2
TH = HB * L
TP = HB * NP
HD = 16
E, INTER = 32, 128
NSH = 2
G, GE, TKG, TOPK = 8, 4, 4, 8
SCALE = 2.5
NEG = -1e18
EPS = 1e-5

IPS = 4
SPH = MC * HB // IPS
NSTEP = 2 * SPH
HPM = 3
MPI = 3
HR = HPM * L
CH = MPI * IPS
PAIR = 2 * L
IW = MPI * HR
DEPTH = 4
WARM_UP, FILL = 4, 16
LAG = 2
ZW = 2 * L - 1
YW = 3 * L - 1
ROW = CH * YW + L
STEP = HR * (ROW + 1)

NE = NSH + E
QD = 5
RING = 4
WE = 3 * 2 * 128

C_BIAS = 0
C_CLS = C_BIAS + MC
C_POS = C_CLS + MC
C_COS = C_POS + MC * L
C_SIN = C_COS + L
C_QM = C_SIN + L
C_OM = C_QM + 8
C_REL = C_OM + 2
C_GW = C_REL + L
C_GB = C_GW + MC * E
C_LOW = C_GB + E
C_EPS = C_LOW + G * G
C_ONE = C_EPS + 1
C_ID = C_ONE + 128
C_ALL = C_ID + 128


def build(nc, emb, cst, rel_v, wattn, wexp, out):
    zd = nc.dram_tensor("rel_scores", (NSTEP, STEP), F32)
    yd = nc.dram_tensor("probs", (NSTEP, STEP), F32)
    cd = nc.dram_tensor("combine", (E, T), F32).ap()

    with ExitStack() as ctx:
        def sem(name):
            return ctx.enter_context(nc.semaphore(name))

        def sb(name, shape, dt=F32, scope=ctx):
            return scope.enter_context(nc.sbuf_tensor(name, shape, dt))

        ps = ctx.enter_context(nc.psum_tensor("ps", [128, 8, 512], F32))

        cs = sb("cs", [128, C_ALL])
        hT = sb("hT", [128, MC, T])
        dT = sb("dT", [128, MC, T])
        sd = sb("sd", [128, T])
        rs = sb("rs", [128, T])
        warm = sb("warm", [128, 4])
        idle = sb("idle", [128, 256])
        xn = sb("xn", [128, MC, T])
        wst = sb("wst", [128, RING, WE])
        whi = sb("whi", [128, RING, WE], F32R)
        wlo = sb("wlo", [128, RING, WE], F32R)
        xhi = sb("xhi", [128, MC, T], F32R)
        xlo = sb("xlo", [128, MC, T], F32R)

        attn = ExitStack()
        wat = sb("wat", [128, 4, MC, D], F32, attn)
        qk = sb("qk", [128, 2, MC, TH], F32, attn)
        qksw = sb("qksw", [128, 2, MC, TH], F32, attn)
        qkc = sb("qkc", [128, 2, MC, TH], F32, attn)
        qrot = sb("qrot", [128, MC, TH], F32, attn)
        ke = sb("ke", [128, MC, B, PAIR], F32, attn)
        ve = sb("ve", [PAIR, B, D], F32, attn)
        zb = sb("zb", [HR, DEPTH, CH, ZW], F32, attn)
        sc = sb("sc", [HR, DEPTH, CH, L], F32, attn)
        rl = sb("rl", [HR, DEPTH, CH, L], F32, attn)
        st_mx = sb("st_mx", [HR, CH], F32, attn)
        st_sum = sb("st_sum", [HR, CH], F32, attn)
        st_inv = sb("st_inv", [HR, DEPTH, CH], F32, attn)
        cth = sb("cth", [128, 2, IPS, L], F32, attn)
        ctxT = sb("ctxT", [128, MC, T], F32, attn)
        first = ExitStack()
        vt = sb("vt", [HR, 6, D], F32, first)
        first.close()
        pt = sb("pt", [PAIR, 2, IPS, IW], F32, attn)
        first = ExitStack()
        em = sb("em", [128, KP, D + 2 * TP], F32, first)
        first.close()
        qbd = sb("qbd", [128, MC, HB, IW], F32, attn)
        yb = sb("yb", [HR, DEPTH, CH, YW], F32, attn)
        attn.close()

        cb = sb("cb", [128, RING, T])
        sg = sb("sg", [128, 2, TH])
        gu = sb("gu", [128, RING, TH])
        ac = sb("ac", [128, RING, TH])
        ahi = sb("ahi", [128, RING, TH], F32R)
        alo = sb("alo", [128, RING, TH], F32R)
        oT = sb("oT", [128, MC, T])
        cT = sb("cT", [E, T])
        NT = T // PAIR
        g_s = sb("g_s", [PAIR, NT, E])
        g_sc = sb("g_sc", [PAIR, NT, E])
        g_pair = sb("g_pair", [PAIR, NT * G, 6])
        g_gs = sb("g_gs", [PAIR, NT, G])
        g_gt = sb("g_gt", [PAIR, NT, G, G])
        g_eq = sb("g_eq", [PAIR, NT, G, G])
        g_rank = sb("g_rank", [PAIR, NT * G])
        g_gm = sb("g_gm", [PAIR, NT * G])
        g_mk = sb("g_mk", [PAIR, NT, E])
        g_top = sb("g_top", [PAIR, NT, TOPK])
        g_rep = sb("g_rep", [PAIR, NT, E])
        g_sel = sb("g_sel", [PAIR, NT, E])
        g_w = sb("g_w", [PAIR, NT, E])
        g_sum = sb("g_sum", [PAIR, NT])
        g_inv = sb("g_inv", [PAIR, NT])
        g_cw = sb("g_cw", [PAIR, NT, E])

        em_in = [sem(f"em_in{c}") for c in range(KP)]
        em2_in = [sem(f"em2_in{c}") for c in range(KP)]
        wat_in = [sem(f"wat_in{m}") for m in range(4)]
        cst_in, relv_in, v_moved = sem("cst_in"), sem("relv_in"), sem("v_moved")
        wt_in = [sem(f"wt_in{s}") for s in range(RING)]
        cb_in = [sem(f"cb_in{s}") for s in range(RING)]
        z_out = [sem(f"z_out{g}") for g in range(NSTEP)]
        z_in = [sem(f"z_in{g}") for g in range(NSTEP)]
        y_out = [sem(f"y_out{g}") for g in range(NSTEP)]
        y_in = [sem(f"y_in{g}") for g in range(NSTEP)]
        comb_out, out_done = sem("comb_out"), sem("out_done")
        proj_done, h_ready = sem("proj_done"), sem("h_ready")
        mean_done, d_ready, sq_ready, var_done = sem("mean_done"), sem("d_ready"), sem("sq_ready"), sem("var_done")
        sd_ready, rs_ready, xn_ready = sem("sd_ready"), sem("rs_ready"), sem("xn_ready")
        qk_done, qk_ready = sem("qk_done"), sem("qk_ready")
        v_done, v_copied = sem("v_done"), sem("v_copied")
        shuf_ready, sin_ready, cos_ready = sem("shuf_ready"), sem("sin_ready"), sem("cos_ready")
        qrot_ready, krot_ready = sem("qrot_ready"), sem("krot_ready")
        qbd_dve, qbd_act, qbd_zero = sem("qbd_dve"), sem("qbd_act"), sem("qbd_zero")
        ke_rel, zmask_ready, y_zero = sem("ke_rel"), sem("zmask_ready"), sem("y_zero")
        score_done, score_copied = sem("score_done"), sem("score_copied")
        sum_ready, max_ready, shift_ready = sem("sum_ready"), sem("max_ready"), sem("shift_ready")
        exp_ready, den_ready, inv_ready, prob_ready = sem("exp_ready"), sem("den_ready"), sem("inv_ready"), sem("prob_ready")
        tr_done, pt_even, pt_odd = sem("tr_done"), sem("pt_even"), sem("pt_odd")
        ctx_done, ctx_half, ctx_ready = sem("ctx_done"), sem("ctx_half"), sem("ctx_ready")
        wo_done, h2_ready = sem("wo_done"), sem("h2_ready")
        xhi_ready, xlo_ready = sem("xhi_ready"), sem("xlo_ready")
        logit_done, sig_ready, route, comb_ready = sem("logit_done"), sem("sig_ready"), sem("route"), sem("comb_ready")
        combT_done, combT_ready = sem("combT_done"), sem("combT_ready")
        ones_ready, warm_done = sem("ones_ready"), sem("warm_done")
        idle_ready = sem("idle_ready")
        whi_ready, wlo_ready = sem("whi_ready"), sem("wlo_ready")
        gate_done, up_done, down_done = sem("gate_done"), sem("up_done"), sem("down_done")
        silu_ready, gu_ready, act_ready = sem("silu_ready"), sem("gu_ready"), sem("act_ready")
        ahi_ready, alo_ready, out_ready = sem("ahi_ready"), sem("alo_ready"), sem("out_ready")

        def half(t):
            return slice(t * TH, (t + 1) * TH)

        def col(a, n):
            return cs[:, a:a + n]

        ident = cs[:, C_ID:C_ID + 128]
        mean_w = cs[:, C_ONE:C_ONE + 128]
        hv = hT[:, :, :].rearrange("p m (b n) -> p m b n", n=L)

        def where(st):
            t, s, q = st // SPH, (st % SPH) // (HB // IPS), st % (HB // IPS)
            return t, s, t * HB + q * IPS

        QK_BANKS = ((4, 2), (6, 0))

        def score_banks(st):
            return 4 + 2 * (st % 2)

        def rows(dram, width, shift, st):
            return bass.AP(dram, st * STEP, [[L * (ROW + shift), HPM], [ROW, L], [1, CH * width]])

        def shifted_rows(dram, width, shift, st, start):
            return bass.AP(dram, st * STEP + start, [[ROW + shift, HR], [width, CH], [1, L]])

        block = ctx.enter_context(nc.Block())

        @block.sync
        def _(sp):
            for c in range(0, KP, 2):
                sp.dma_start(em[:, c, 0:D + TP], emb[c][:, 0:D + TP]).then_inc(em_in[c], 16)
            sp.dma_start(wat[:, 0, :, :], wattn[:, 0, :, :]).then_inc(wat_in[0], 16)
            for c in range(0, KP, 2):
                sp.dma_start(em[:, c, D + TP:D + 2 * TP], emb[c][:, D + TP:D + 2 * TP]).then_inc(em2_in[c], 16)
            for mat in range(1, 4):
                sp.dma_start(wat[:, mat, :, :], wattn[:, mat, :, :]).then_inc(wat_in[mat], 16)
            for n in range(RING):
                sp.dma_start(wst[:, n, :], wexp[n]).then_inc(wt_in[n], 16)

            def scores_in(st):
                sp.wait_ge(z_out[st], 16)
                if st >= DEPTH:
                    sp.wait_ge(sum_ready, st - DEPTH + 1)
                sp.dma_start(rl[:, st % DEPTH, :, :], shifted_rows(zd, ZW, -1, st, L - 1)).then_inc(z_in[st], 16)

            def probs_out(st):
                sp.wait_ge(prob_ready, st + 1)
                sp.dma_start(rows(yd, YW, 1, st), yb[:, st % DEPTH, :, :].rearrange("p c k -> p (c k)")).then_inc(y_out[st], 16)

            def probs_in(st):
                sp.wait_ge(y_out[st], 16)
                sp.dma_start(yb[:, st % DEPTH, :, YW - L:YW], shifted_rows(yd, YW, 1, st, 0)).then_inc(y_in[st], 16)

            for st in range(DEPTH):
                scores_in(st)
                if st == 2:
                    probs_out(0)
            sp.wait_ge(v_copied, 6)
            for r in range(3):
                n = (B - r + 2) // 3
                sp.dma_start(ve[0:L, r:B:3, :], vt[r * L:(r + 1) * L, 0:n, :]).then_inc(v_moved, 16)
            for st in range(1, DEPTH):
                probs_in(st - 1)
                probs_out(st)
            for i in range(DEPTH, NSTEP + 1):
                if i < NSTEP:
                    scores_in(i)
                if i != DEPTH + 1:
                    probs_in(i - 1 if i == DEPTH else i - 2)
                if i > DEPTH:
                    probs_out(i - 1)
            probs_in(NSTEP - 1)

            def weights(n, slot):
                sp.wait_ge(whi_ready, n - RING + 1)
                sp.wait_ge(wlo_ready, n - RING + 1)
                sp.dma_start(wst[:, slot, :], wexp[n] if type(n) is int else
                             wexp[bass.ds(n, 1)].rearrange("o p w -> (o p) w")).then_inc(wt_in[slot], 16)

            def combine(n, slot):
                sp.wait_ge(act_ready, 2 * (n - RING) + 3)
                row = cd[n - NSH:n - NSH + 1, :] if type(n) is int else cd[bass.ds(n - NSH, 1), :]
                sp.dma_start(cb[:, slot, :], row.broadcast_to([128, T])).then_inc(cb_in[slot], 16)

            weights(RING, 0)
            sp.wait_ge(combT_ready, 2)
            sp.dma_start(cd, cT[:, :]).then_inc(comb_out, 16)
            sp.wait_ge(comb_out, 16)

            for n in range(NSH, RING):
                sp.dma_start(cb[:, n, :], cd[n - NSH:n - NSH + 1, :].broadcast_to([128, T])).then_inc(cb_in[n], 16)
            with sp.Fori(0, (NE - 2 - RING) // RING) as turn_of_ring:
                n0 = turn_of_ring * RING + RING
                for k in range(RING):
                    combine(n0 + k, k)
                    weights(n0 + k + 1, (k + 1) % RING)
            combine(NE - 2, (NE - 2) % RING)
            weights(NE - 1, (NE - 1) % RING)
            combine(NE - 1, (NE - 1) % RING)
            for t in range(2):
                sp.wait_ge(out_ready, MC * (t + 1))
                sp.dma_start(out.rearrange("m p t -> p m t")[:, :, half(t)], oT[:, :, half(t)]).then_inc(out_done, 16)
            sp.wait_ge(out_done, 32)

        @block.tensor
        def _(pe):
            def mean(t, bank):
                for m in range(MC):
                    mm = nc.tensor.matmul(ps[:, bank, 0:TH], mean_w, hT[:, m, half(t)],
                                          start=(m == 0), stop=(m == MC - 1))
                mm.then_inc(mean_done, 1)

            def variance(k, t, bank):
                pe.wait_ge(sq_ready, 2 * k + t + 1)
                for m in range(MC):
                    mm = nc.tensor.matmul(ps[:, bank, 0:TH], mean_w, xn[:, m, half(t)],
                                          start=(m == 0), stop=(m == MC - 1))
                mm.then_inc(var_done, 1)

            def query_key(t, mat):
                bank = QK_BANKS[t][mat]
                for s in range(MC):
                    for m in range(MC):
                        mm = nc.tensor.matmul(ps[:, bank + s, 0:TH],
                                              wat[:, mat, m, s * 128:(s + 1) * 128], dT[:, m, half(t)],
                                              start=(m == 0), stop=(m == MC - 1))
                mm.then_inc(qk_done, 1)

            def keep_clock(count, bank):
                for _ in range(count):
                    nc.tensor.matmul(ps[:, bank, 0:256], idle[:, 0:128], idle[:, :], start=True, stop=True)

            def embed(t, arrived, chunks):
                for c in chunks:
                    pe.wait_ge(arrived[c], 16)
                    for m in range(MC):
                        mm = nc.tensor.matmul(ps[:, 4 + 2 * t + m, 0:TP], em[:, c, m * 128:(m + 1) * 128],
                                              em[:, c, D + t * TP:D + (t + 1) * TP],
                                              start=(c == 0), stop=(c == KP - 1))
                        if c == KP - 1:
                            mm.then_inc(proj_done, 1)

            pe.wait_ge(idle_ready, 1)
            keep_clock(WARM_UP, 0)
            embed(0, em_in, range(KP))
            embed(1, em2_in, range(0, 2))
            pe.wait_ge(cst_in, 16)
            pe.wait_ge(h_ready, 2 * MC)
            mean(0, 0)
            embed(1, em2_in, range(2, 4))
            pe.wait_ge(wat_in[0], 16)
            pe.wait_ge(d_ready, 1)
            query_key(0, 0)
            variance(0, 0, 0)
            pe.wait_ge(wat_in[1], 16)
            query_key(0, 1)
            embed(1, em2_in, range(4, KP))
            pe.wait_ge(h_ready, 3 * MC)
            mean(1, 1)
            pe.wait_ge(d_ready, 2)
            query_key(1, 0)
            variance(0, 1, 1)
            pe.wait_ge(sd_ready, 2)
            query_key(1, 1)

            def values():
                pe.wait_ge(wat_in[2], 16)
                pe.wait_ge(xn_ready, 2)
                pe.wait_ge(qk_ready, 4)
                for i in range(6):
                    n = min(HR, T - i * HR)
                    for m in range(MC):
                        mm = nc.tensor.matmul(ps[0:n, i // 2, (i % 2) * D:(i % 2 + 1) * D],
                                              xn[:, m, i * HR:i * HR + n], wat[:, 2, m, :],
                                              start=(m == 0), stop=(m == MC - 1))
                    if i % 2:
                        mm.then_inc(v_done, 1)

            def scores_wait(st):
                t, s, b0 = where(st)
                if st == 0:
                    pe.wait_ge(ke_rel, MC)
                    pe.wait_ge(qk_ready, 1)
                    pe.wait_ge(qbd_zero, 1)
                if st == 1:
                    pe.wait_ge(qk_ready, 3)
                if st % SPH == 0:
                    pe.wait_ge(krot_ready, t + 1)
                if st % (HB // IPS) == 0:
                    pe.wait_ge(qbd_dve, QD * (MC * t + s + 1))
                    pe.wait_ge(qbd_act, (8 - QD) * (MC * t + s + 1))
                if st >= 2:
                    pe.wait_ge(score_copied, 2 * (st - 1))

            def scores_image(st, i):
                    t, s, b0 = where(st)
                    for m in range(MPI):
                        c = i * MPI + m
                        mm = nc.tensor.matmul(
                            ps[0:HR, score_banks(st) + c // 6, (c % 6) * PAIR:(c % 6 + 1) * PAIR],
                            qbd[:, s, b0 % HB + i, m * HR:(m + 1) * HR], ke[:, s, b0 + i, :],
                            start=True, stop=True)
                    if i == IPS - 1:
                        mm.then_inc(score_done, 1)

            def turn_wait(st):
                pe.wait_ge(y_in[st], 16)
                if st == 0:
                    pe.wait_ge(v_copied, 6)

            def turn_image(st, i):
                    u = st * IPS + i
                    if u >= 2:
                        pe.wait_ge(pt_odd if u % 2 else pt_even, u // 2)
                    for m in range(MPI):
                        mm = nc.tensor.transpose(ps[0:PAIR, u % 2, m * HR:(m + 1) * HR],
                                                 yb[:, st % DEPTH, i * MPI + m, L - 1:YW], ident[0:HR, 0:HR])
                    mm.then_inc(tr_done, 1)

            def context_wait(st):
                pe.wait_ge(pt_even, 2 * (st + 1))
                pe.wait_ge(pt_odd, 2 * (st + 1))
                if st == 0:
                    pe.wait_ge(relv_in, 16)
                    pe.wait_ge(v_moved, 48)
                if st >= 2:
                    pe.wait_ge(ctx_ready, st - 1)

            def context_image(st, i):
                    t, s, b0 = where(st)
                    for j in range(4):
                        mm = nc.tensor.matmul(ps[32 * j:32 * j + 32, 2 + st % 2, i * PAIR:(i + 1) * PAIR],
                                              ve[:, b0 + i, s * 128 + 32 * j:s * 128 + 32 * j + 32],
                                              pt[:, st % 2, i, j * PAIR:(j + 1) * PAIR], start=True, stop=True)
                    if i == IPS - 1:
                        mm.then_inc(ctx_done, 1)

            def project(t, bank):
                pe.wait_ge(ctx_ready, SPH * (t + 1))
                pe.wait_ge(wat_in[3], 16)
                for m in range(MC):
                    for s in range(MC):
                        mm = nc.tensor.matmul(ps[:, bank + m, 0:TH], wat[:, 3, s, m * 128:(m + 1) * 128],
                                              ctxT[:, s, half(t)], start=(s == 0), stop=(s == MC - 1))
                    mm.then_inc(wo_done, 1)

            for i in range(NSTEP + DEPTH + 1):
                if i == DEPTH + SPH + 2:
                    pe.wait_ge(h2_ready, MC)
                    mean(0, 6)
                if i == DEPTH + SPH + 3:
                    variance(1, 0, 7)
                if i < NSTEP:
                    scores_wait(i)
                if 0 <= i - DEPTH < NSTEP:
                    turn_wait(i - DEPTH)
                if 0 <= i - DEPTH - 1 < NSTEP:
                    context_wait(i - DEPTH - 1)
                for k in range(IPS):
                    if 0 <= i - DEPTH < NSTEP:
                        turn_image(i - DEPTH, k)
                    if i == DEPTH + SPH + 1 and k == 1:
                        pe.wait_ge(score_copied, 2 * NSTEP)
                        project(0, 4)
                    if i < NSTEP:
                        scores_image(i, k)
                    if 0 <= i - DEPTH - 1 < NSTEP:
                        context_image(i - DEPTH - 1, k)
                if i == DEPTH - 1:
                    values()
                    keep_clock(FILL, 3)

            def gate_up(n, slot, t, pair_free):
                if t == 0:
                    pe.wait_ge(whi_ready, n + 1)
                    pe.wait_ge(wlo_ready, n + 1)
                if pair_free is not None:
                    pe.wait_ge(gu_ready, pair_free)
                for mat, done in ((0, gate_done), (1, up_done)):
                    k = 0
                    for m in range(MC):
                        a = (2 * mat + m) * 128
                        for w, x in ((whi, xhi), (whi, xlo), (wlo, xhi)):
                            mm = nc.tensor.matmul(ps[:, 2 * t + mat, 0:TH], w[:, slot, a:a + 128],
                                                  x[:, m, half(t)], start=(k == 0), stop=(k == 3 * MC - 1))
                            k += 1
                    mm.then_inc(done, 1)

            def down(u, slot, r, t, start=False, stop=False):
                pe.wait_ge(ahi_ready, u + 1)
                pe.wait_ge(alo_ready, u + 1)
                for m in range(MC):
                    a = (4 + m) * 128
                    for k, (w, x) in enumerate(((whi, ahi), (whi, alo), (wlo, ahi))):
                        mm = nc.tensor.matmul(ps[:, 4 + 2 * t + m, 0:TH], w[:, slot, a:a + 128], x[:, r, :],
                                              start=(start and k == 0), stop=(stop and k == 2),
                                              skip_group_check=True)
                mm.then_inc(down_done, 1)

            def logits(t):
                pe.wait_ge(xn_ready, 2 + t + 1)
                for i in range(NT // 2 * t, NT // 2 * (t + 1)):
                    for m in range(MC):
                        mm = nc.tensor.matmul(ps[0:PAIR, 7, i * E:(i + 1) * E], xn[:, m, i * PAIR:(i + 1) * PAIR],
                                              cs[:, C_GW + m * E:C_GW + (m + 1) * E],
                                              start=(m == 0), stop=(m == MC - 1))
                mm.then_inc(logit_done, 1)

            pe.wait_ge(xhi_ready, 1)
            pe.wait_ge(xlo_ready, 1)
            pe.wait_ge(pt_even, 2 * NSTEP)
            pe.wait_ge(pt_odd, 2 * NSTEP)
            gate_up(0, 0, 0, None)
            project(1, 2)
            gate_up(1, 1, 0, 1)
            pe.wait_ge(h2_ready, 2 * MC)
            pe.wait_ge(d_ready, 3)
            mean(1, 6)
            down(0, 0, 0, 0, start=True)
            gate_up(2, 2, 0, 2)
            pe.wait_ge(sd_ready, 3)
            variance(1, 1, 7)
            down(1, 1, 1, 0)
            gate_up(3, 3, 0, 3)
            pe.wait_ge(sd_ready, 4)
            logits(0)
            logits(1)
            pe.wait_ge(xhi_ready, 2)
            pe.wait_ge(xlo_ready, 2)
            gate_up(0, 0, 1, None)
            gate_up(1, 1, 1, 5)
            pe.wait_ge(sig_ready, 1)
            down(2, 0, 2, 1, start=True)
            gate_up(2, 2, 1, 6)
            down(3, 1, 3, 1)
            pe.wait_ge(comb_ready, 1)
            pe.wait_ge(gu_ready, 4)
            for i in range(NT):
                mm = nc.tensor.transpose(ps[0:E, i // 4, (i % 4) * PAIR:(i % 4 + 1) * PAIR], g_cw[:, i, :],
                                         ident[0:PAIR, 0:PAIR])
            mm.then_inc(combT_done, 1)
            gate_up(3, 3, 1, 7)
            pe.wait_ge(combT_ready, 2)

            def expert(n, slot):
                for t in range(2):
                    gate_up(n, slot, t, 2 * n + t - 1)
                    down(2 * (n - 2) + t, (slot - 2) % RING, (2 * slot + t) % RING, t)

            with pe.Fori(0, (NE - 2 - RING) // RING) as turn_of_ring:
                n0 = turn_of_ring * RING + RING
                for k in range(RING):
                    expert(n0 + k, k)
            for n in range(NE - 2, NE):
                expert(n, n % RING)
            for n in range(NE - 2, NE):
                for t in range(2):
                    down(2 * n + t, n % RING, (2 * n + t) % RING, t, stop=(n == NE - 1))

        @block.vector
        def _(dve):
            nc.vector.memset(idle[:, :], 0.0).then_inc(idle_ready, 1)
            dve.wait_ge(cst_in, 16)
            for m in range(MC):
                nc.vector.tensor_tensor(hv[:, m, :, 0], col(C_CLS + m, 1).broadcast_to([128, B]),
                                        col(C_POS + m * L, 1).broadcast_to([128, B]), ALU.add).then_inc(h_ready, 1)

            def centre(k, t, bank):
                dve.wait_ge(mean_done, 2 * k + t + 1)
                nc.vector.tensor_tensor(dT[:, :, half(t)], hT[:, :, half(t)],
                                        ps[:, bank, 0:TH].unsqueeze(1).broadcast_to([128, MC, TH]),
                                        ALU.subtract).then_inc(d_ready, 1)

            def deviation(k, t):
                dve.wait_ge(sd_ready, 2 * k + t + 1)
                nc.vector.reciprocal(rs[:, half(t)], sd[:, half(t)]).then_inc(rs_ready, 1)
                dve.wait_ge(rs_ready, 2 * k + t + 1)

            def embed(t):
                for m in range(MC):
                    dve.wait_ge(proj_done, 2 * t + m + 1)
                    nc.vector.scalar_tensor_tensor(
                        out=hv[:, m, t * HB:(t + 1) * HB, 1:L],
                        in0=ps[:, 4 + 2 * t + m, 0:TP].rearrange("p (b n) -> p b n", n=NP),
                        scalar=col(C_BIAS + m, 1),
                        in1=cs[:, C_POS + m * L + 1:C_POS + (m + 1) * L].unsqueeze(1).broadcast_to([128, HB, NP]),
                        op0=ALU.add, op1=ALU.add).then_inc(h_ready, 1)
            embed(0)
            centre(0, 0, 0)

            swap = [i ^ 1 for i in range(32)]

            def divide(t):
                deviation(0, t)
                if t == 1:
                    dve.wait_ge(cos_ready, 1)
                for mat in range(2):
                    dve.wait_ge(qk_done, 2 * t + mat + 1)
                    nc.vector.tensor_tensor(qk[:, mat, :, :], ps[:, QK_BANKS[t][mat]:QK_BANKS[t][mat] + 2, 0:TH],
                                            rs[:, half(t)].unsqueeze(1).broadcast_to([128, MC, TH]),
                                            ALU.mult).then_inc(qk_ready, 1)
                dve.wait_ge(qk_ready, 2 * t + 2)
                nc.vector.stream_shuffle(qksw[:, :, :, :], qk[:, :, :, :], swap).then_inc(shuf_ready, 1)

            def sine(t):
                dve.wait_ge(shuf_ready, t + 1)
                v = qksw[:, :, :, :].rearrange("p a s (b n) -> p (a s b) n", n=L)
                nc.vector.tensor_tensor(v, v, col(C_SIN, L).unsqueeze(1).broadcast_to([128, 4 * HB, L]),
                                        ALU.mult).then_inc(sin_ready, 1)

            def rotated(t):
                dve.wait_ge(sin_ready, t + 1)
                dve.wait_ge(cos_ready, t + 1)
                if t == 1:
                    dve.wait_ge(qbd_act, (8 - QD) * MC)
                nc.vector.tensor_tensor(qrot[:, :, :], qksw[:, 0, :, :], qkc[:, 0, :, :],
                                        ALU.add).then_inc(qrot_ready, 1)
                nc.vector.tensor_tensor(ke[:, :, t * HB:(t + 1) * HB, 0:L],
                                        qksw[:, 1, :, :].rearrange("p s (b n) -> p s b n", n=L),
                                        qkc[:, 1, :, :].rearrange("p s (b n) -> p s b n", n=L),
                                        ALU.add).then_inc(krot_ready, 1)

            def block_diagonal(t, s):
                dve.wait_ge(qrot_ready, t + 1)
                if t == 1:
                    dve.wait_ge(score_done, 2 * (s + 1))
                for h in range(QD):
                    nc.vector.tensor_scalar(qbd[:, s, :, h * L:(h + 1) * L],
                                            qrot[:, s, :].rearrange("p (b n) -> p b n", n=L),
                                            col(C_QM + h, 1), None, ALU.mult).then_inc(qbd_dve, 1)

            divide(0)
            embed(1)
            sine(0)
            centre(0, 1, 1)
            rotated(0)
            block_diagonal(0, 0)
            divide(1)
            block_diagonal(0, 1)
            sine(1)
            rotated(1)

            def softmax_top(st):
                x = sc[:, st % DEPTH, :, :]
                dve.wait_ge(z_in[st], 16)
                dve.wait_ge(score_copied, 2 * (st + 1))
                nc.vector.tensor_tensor(x, x, rl[:, st % DEPTH, :, :], ALU.add).then_inc(sum_ready, 1)
                dve.wait_ge(sum_ready, st + 1)
                nc.vector.tensor_reduce(st_mx[:, :], x, AX_X, ALU.max).then_inc(max_ready, 1)
                dve.wait_ge(max_ready, st + 1)
                nc.vector.tensor_tensor(x, x, st_mx[:, :].unsqueeze(2).broadcast_to([HR, CH, L]),
                                        ALU.subtract).then_inc(shift_ready, 1)

            def softmax_bottom(st):
                dve.wait_ge(exp_ready, st + 1)
                nc.vector.tensor_reduce(st_sum[:, :], sc[:, st % DEPTH, :, :], AX_X, ALU.add).then_inc(den_ready, 1)
                dve.wait_ge(den_ready, st + 1)
                if st >= DEPTH:
                    dve.wait_ge(prob_ready, st - DEPTH + 1)
                nc.vector.reciprocal(st_inv[:, st % DEPTH, :], st_sum[:, :]).then_inc(inv_ready, 1)

            def turn_copy(st, i):
                u = st * IPS + i
                dve.wait_ge(tr_done, u + 1)
                if st == 0:
                    dve.wait_ge(v_moved, 48)
                if st >= 2:
                    dve.wait_ge(ctx_done, st - 1)
                nc.vector.tensor_copy(pt[:, st % 2, i, :], ps[0:PAIR, u % 2, 0:IW]).then_inc(pt_odd, 1)

            def context_add(st):
                t, s, b0 = where(st)
                dve.wait_ge(ctx_half, st + 1)
                nc.vector.scalar_tensor_tensor(
                    out=ctxT[:, s, b0 * L:(b0 + IPS) * L].rearrange("p (i q) -> p i q", q=L),
                    in0=ps[:, 2 + st % 2, 0:IPS * PAIR].rearrange("p (i k) -> p i k", k=PAIR)[:, :, L:PAIR],
                    scalar=col(C_OM + 1, 1), in1=cth[:, st % 2, :, :],
                    op0=ALU.mult, op1=ALU.add).then_inc(ctx_ready, 1)

            def residual(t, bank):
                for m in range(MC):
                    dve.wait_ge(wo_done, 2 * t + m + 1)
                    nc.vector.tensor_tensor(hT[:, m, half(t)], hT[:, m, half(t)], ps[:, bank + m, 0:TH],
                                            ALU.add).then_inc(h2_ready, 1)

            def normalise(t):
                deviation(1, t)
                nc.vector.tensor_tensor(xn[:, :, half(t)], dT[:, :, half(t)],
                                        rs[:, half(t)].unsqueeze(1).broadcast_to([128, MC, TH]),
                                        ALU.mult).then_inc(xn_ready, 1)

            def split_x(t):
                dve.wait_ge(xhi_ready, t + 1)
                nc.vector.tensor_tensor(xlo[:, :, half(t)], xn[:, :, half(t)],
                                        xhi[:, :, half(t)].bitcast(F32), ALU.subtract).then_inc(xlo_ready, 1)

            def split_low(n, slot, slot_free=None):
                dve.wait_ge(whi_ready, n + 1)
                if slot_free is not None:
                    dve.wait_ge(down_done, slot_free)
                nc.vector.tensor_tensor(wlo[:, slot, :], wst[:, slot, :], whi[:, slot, :].bitcast(F32),
                                        ALU.subtract).then_inc(wlo_ready, 1)

            for s in range(MC):
                block_diagonal(1, s)
            for st in range(DEPTH):
                softmax_top(st)
                softmax_bottom(st)
            for i in range(DEPTH, NSTEP + DEPTH + 1):
                st_turn, st_soft, st_ctx = i - DEPTH, i - LAG, i - DEPTH - 1
                first = i > NSTEP
                if first and st_soft < NSTEP:
                    softmax_top(st_soft)
                    softmax_bottom(st_soft)
                if 0 <= st_turn < NSTEP:
                    turn_copy(st_turn, 1)
                if not first and DEPTH <= st_soft:
                    softmax_top(st_soft)
                if 0 <= st_turn < NSTEP:
                    turn_copy(st_turn, 3)
                if not first and DEPTH <= st_soft:
                    softmax_bottom(st_soft)
                if i == DEPTH + SPH + 1:
                    residual(0, 4)
                if i == DEPTH + SPH + 2:
                    centre(1, 0, 6)
                if 0 <= st_ctx < NSTEP:
                    context_add(st_ctx)
                if DEPTH + SPH + 1 <= i <= DEPTH + SPH + NSH + 1:
                    split_low(i - DEPTH - SPH - 1, i - DEPTH - SPH - 1)
                if i == DEPTH + SPH + 3:
                    normalise(0)
                    split_x(0)

            def gate_times_up(u, t, r, ring_free=None):
                dve.wait_ge(silu_ready, u + 1)
                dve.wait_ge(up_done, u + 1)
                if ring_free is not None:
                    dve.wait_ge(act_ready, ring_free)
                nc.vector.tensor_tensor(gu[:, r, :], sg[:, t, :], ps[:, 2 * t + 1, 0:TH],
                                        ALU.mult).then_inc(gu_ready, 1)

            def act_low(u, r, ring_free=None):
                dve.wait_ge(ahi_ready, u + 1)
                if ring_free is not None:
                    dve.wait_ge(down_done, ring_free)
                nc.vector.tensor_tensor(alo[:, r, :], ac[:, r, :], ahi[:, r, :].bitcast(F32),
                                        ALU.subtract).then_inc(alo_ready, 1)

            count = [0]

            def routed(ins):
                count[0] += 1
                ins.then_inc(route, 1)
                dve.wait_ge(route, count[0])

            def route_groups():
                dve.wait_ge(sig_ready, 1)
                routed(nc.vector.tensor_tensor(g_sc[:, :, :], g_s[:, :, :],
                                               cs[0:PAIR, C_GB:C_GB + E].unsqueeze(1).broadcast_to([PAIR, NT, E]),
                                               ALU.add))
                q = g_sc[:, :, :].rearrange("p t (g e) -> p (t g) e", e=GE)
                nc.vector.tensor_tensor(g_pair[:, :, 0:3], q[:, :, 0:3], q[:, :, 1:4], ALU.add)
                nc.vector.tensor_tensor(g_pair[:, :, 3:5], q[:, :, 0:2], q[:, :, 2:4], ALU.add)
                routed(nc.vector.tensor_tensor(g_pair[:, :, 5:6], q[:, :, 0:1], q[:, :, 3:4], ALU.add))
                routed(nc.vector.tensor_reduce(g_gs[:, :, :].rearrange("p t g -> p (t g)"), g_pair[:, :, :],
                                               AX_X, ALU.max))

            def route_masked():
                mine = g_gs[:, :, :].unsqueeze(3).broadcast_to([PAIR, NT, G, G])
                other = g_gs[:, :, :].unsqueeze(2).broadcast_to([PAIR, NT, G, G])
                low = cs[0:PAIR, C_LOW:C_LOW + G * G].rearrange("p (g h) -> p g h", h=G)
                nc.vector.tensor_tensor(g_gt[:, :, :, :], other, mine, ALU.is_gt)
                routed(nc.vector.tensor_tensor(g_eq[:, :, :, :], other, mine, ALU.is_equal))
                routed(nc.vector.tensor_tensor(g_eq[:, :, :, :], g_eq[:, :, :, :],
                                               low.unsqueeze(1).broadcast_to([PAIR, NT, G, G]), ALU.mult))
                routed(nc.vector.tensor_tensor(g_gt[:, :, :, :], g_gt[:, :, :, :], g_eq[:, :, :, :], ALU.add))
                routed(nc.vector.tensor_reduce(g_rank[:, :], g_gt[:, :, :, :].rearrange("p t g h -> p (t g) h"),
                                               AX_X, ALU.add))
                routed(nc.vector.tensor_scalar(g_gm[:, :], g_rank[:, :], TKG - 0.5, None, ALU.is_lt))
                routed(nc.vector.tensor_tensor(g_mk[:, :, :].rearrange("p t (g e) -> p (t g) e", e=GE),
                                               g_sc[:, :, :].rearrange("p t (g e) -> p (t g) e", e=GE),
                                               g_gm[:, :].unsqueeze(2).broadcast_to([PAIR, NT * G, GE]), ALU.mult))

            def route_top():
                for i in range(NT):
                    ins = nc.vector.max(g_top[:, i, :], g_mk[:, i, :])
                routed(ins)
                for i in range(NT):
                    ins = nc.vector.match_replace(g_rep[:, i, :], g_top[:, i, :], g_mk[:, i, :], -3e38)
                routed(ins)

            def route_weights():
                routed(nc.vector.tensor_tensor(g_sel[:, :, :], g_rep[:, :, :], g_mk[:, :, :], ALU.not_equal))
                routed(nc.vector.tensor_tensor(g_w[:, :, :], g_s[:, :, :], g_sel[:, :, :], ALU.mult))
                routed(nc.vector.tensor_reduce(g_sum[:, :], g_w[:, :, :], AX_X, ALU.add))
                routed(nc.vector.tensor_scalar(g_sum[:, :], g_sum[:, :], 1e-20, None, ALU.add))
                routed(nc.vector.reciprocal(g_inv[:, :], g_sum[:, :]))
                routed(nc.vector.tensor_scalar(g_inv[:, :], g_inv[:, :], SCALE, None, ALU.mult))
                nc.vector.tensor_tensor(g_cw[:, :, :], g_w[:, :, :],
                                        g_inv[:, :].unsqueeze(2).broadcast_to([PAIR, NT, E]),
                                        ALU.mult).then_inc(comb_ready, 1)

            residual(1, 2)
            gate_times_up(0, 0, 0)
            split_low(3, 3)
            gate_times_up(1, 0, 1)
            centre(1, 1, 6)
            act_low(0, 0)
            act_low(1, 1)
            gate_times_up(2, 0, 2)
            normalise(1)
            split_x(1)
            route_groups()
            gate_times_up(3, 0, 3)
            gate_times_up(4, 1, 0, 1)
            route_masked()
            gate_times_up(5, 1, 1, 2)
            act_low(2, 2)
            route_top()
            act_low(3, 3)
            route_weights()
            gate_times_up(6, 1, 2, 5)
            split_low(RING, 0, 4)
            gate_times_up(7, 1, 3, 7)
            for t in range(2):
                act_low(2 * NSH + t, t, t + 1)

            def expert(n, slot, last):
                if not last:
                    split_low(n + 1, (slot + 1) % RING, 2 * (n + 1 - RING) + 2)
                for t in range(2):
                    u = 2 * n + t
                    gate_times_up(u, t, (2 * slot + t) % RING, u - RING + 1)
                    act_low(u - 2, (2 * slot + 2 + t) % RING, u - 2 - RING + 1)

            with dve.Fori(0, (NE - 2 - RING) // RING) as turn_of_ring:
                n0 = turn_of_ring * RING + RING
                for k in range(RING):
                    expert(n0 + k, k, False)
            for n in range(NE - 2, NE):
                expert(n, n % RING, n == NE - 1)
            for t in range(2):
                u = 2 * (NE - 1) + t
                act_low(u, u % RING, u - RING + 1)
            for t in range(2):
                dve.wait_ge(down_done, 2 * NE - 1 + t)
                for m in range(MC):
                    nc.vector.tensor_tensor(oT[:, m, half(t)], hT[:, m, half(t)], ps[:, 4 + 2 * t + m, 0:TH],
                                            ALU.add).then_inc(out_ready, 1)

        @block.scalar
        def _(act):
            act.dma_start(cs[:, :], cst).then_inc(cst_in, 16)
            for c in range(1, KP, 2):
                act.dma_start(em[:, c, 0:D + TP], emb[c][:, 0:D + TP]).then_inc(em_in[c], 16)
            for c in range(1, KP, 2):
                act.dma_start(em[:, c, D + TP:D + 2 * TP], emb[c][:, D + TP:D + 2 * TP]).then_inc(em2_in[c], 16)
            act.dma_start(ve[L:PAIR, :, :], rel_v.unsqueeze(1).broadcast_to([L, B, D])).then_inc(relv_in, 16)

            def squares(k, t):
                act.wait_ge(d_ready, 2 * k + t + 1)
                nc.scalar.activation(xn[:, :, half(t)], dT[:, :, half(t)], ACT.Square).then_inc(sq_ready, 1)

            def root(k, t, bank):
                act.wait_ge(var_done, 2 * k + t + 1)
                nc.scalar.activation(sd[:, half(t)], ps[:, bank, 0:TH], ACT.Sqrt,
                                     bias=col(C_EPS, 1)).then_inc(sd_ready, 1)

            def load_table(k, function):
                nc.scalar.activation(warm[:, k:k + 1], col(C_EPS, 1), function).then_inc(warm_done, 1)

            act.wait_ge(cst_in, 16)
            load_table(0, ACT.Sqrt)
            for t in range(2):
                squares(0, t)
                root(0, t, t)
            load_table(1, ACT.Exp)

            def block_diagonal(t, s):
                act.wait_ge(qrot_ready, t + 1)
                if t == 1:
                    act.wait_ge(score_done, 2 * (s + 1))
                for h in range(QD, 8):
                    nc.scalar.activation(qbd[:, s, :, h * L:(h + 1) * L],
                                         qrot[:, s, :].rearrange("p (b n) -> p b n", n=L), ACT.Copy,
                                         scale=col(C_QM + h, 1)).then_inc(qbd_act, 1)

            def copy_scores(st):
                act.wait_ge(score_done, st + 1)
                if st >= DEPTH:
                    act.wait_ge(prob_ready, st - DEPTH + 1)
                    act.wait_ge(z_out[st - DEPTH], 16)
                src = ps[0:HR, score_banks(st):score_banks(st) + 2, 0:6 * PAIR].rearrange(
                    "p a (c k) -> p a c k", k=PAIR)
                for dst, k in ((zb, L), (sc, 0)):
                    nc.scalar.copy(dst[:, st % DEPTH, :, 0:L].rearrange("p (a c) k -> p a c k", a=2),
                                   src[:, :, :, k:k + L]).then_inc(score_copied, 1)
                    if dst is zb:
                        if st == 0:
                            act.wait_ge(zmask_ready, 1)
                        act.wait_ge(score_copied, 2 * st + 1)
                        act.dma_start(rows(zd, ZW, -1, st),
                                      zb[:, st % DEPTH, :, :].rearrange("p c k -> p (c k)")).then_inc(z_out[st], 16)

            def exponent(st):
                act.wait_ge(shift_ready, st + 1)
                nc.scalar.activation(sc[:, st % DEPTH, :, :], sc[:, st % DEPTH, :, :], ACT.Exp).then_inc(exp_ready, 1)

            def turn_copy(st, i):
                u = st * IPS + i
                act.wait_ge(tr_done, u + 1)
                if st == 0:
                    act.wait_ge(v_moved, 48)
                if st >= 2:
                    act.wait_ge(ctx_done, st - 1)
                nc.scalar.copy(pt[:, st % 2, i, :], ps[0:PAIR, u % 2, 0:IW]).then_inc(pt_even, 1)

            def context_half(st):
                act.wait_ge(ctx_done, st + 1)
                if st >= 2:
                    act.wait_ge(ctx_ready, st - 1)
                nc.scalar.activation(cth[:, st % 2, :, :],
                                     ps[:, 2 + st % 2, 0:IPS * PAIR].rearrange(
                                         "p (i k) -> p i k", k=PAIR)[:, :, 0:L],
                                     ACT.Copy, scale=col(C_OM, 1)).then_inc(ctx_half, 1)

            def split_x(t):
                act.wait_ge(xn_ready, 2 + t + 1)
                nc.scalar.copy(xhi[:, :, half(t)], xn[:, :, half(t)]).then_inc(xhi_ready, 1)

            def split_high(n, slot, slot_free=None):
                act.wait_ge(wt_in[slot], 4 * (n - slot) + 16)
                if slot_free is not None:
                    act.wait_ge(down_done, slot_free)
                nc.scalar.copy(whi[:, slot, :], wst[:, slot, :]).then_inc(whi_ready, 1)

            for s in range(MC):
                block_diagonal(0, s)
            for st in range(DEPTH):
                copy_scores(st)
                if st % 2:
                    block_diagonal(1, st // 2)
            for k in range(6):
                n = min(HR, T - k * HR)
                act.wait_ge(v_done, k // 2 + 1)
                nc.scalar.copy(vt[0:n, k, :], ps[0:n, k // 2, (k % 2) * D:(k % 2 + 1) * D]).then_inc(v_copied, 1)
            for st in range(DEPTH):
                exponent(st)
            for i in range(DEPTH, NSTEP + DEPTH + 1):
                st_turn, st_soft, st_ctx = i - DEPTH, i - LAG, i - DEPTH - 1
                if DEPTH + LAG <= i <= NSTEP:
                    turn_copy(st_turn, 0)
                    exponent(st_soft)
                    turn_copy(st_turn, 2)
                else:
                    if i > NSTEP and st_soft < NSTEP:
                        exponent(st_soft)
                    for k in range(0, IPS, 2):
                        if 0 <= st_turn < NSTEP:
                            turn_copy(st_turn, k)
                if DEPTH <= i < NSTEP:
                    copy_scores(i)
                if DEPTH + SPH + 1 <= i <= DEPTH + SPH + NSH + 1:
                    split_high(i - DEPTH - SPH - 1, i - DEPTH - SPH - 1)
                if i == DEPTH + SPH + 2:
                    squares(1, 0)
                if 0 <= st_ctx < NSTEP:
                    context_half(st_ctx)
                if i == DEPTH + SPH + 3:
                    root(1, 0, 7)
                    split_x(0)

            def silu(u, t, sg_free=None):
                act.wait_ge(gate_done, u + 1)
                if sg_free is not None:
                    act.wait_ge(gu_ready, sg_free)
                nc.scalar.activation(sg[:, t, :], ps[:, 2 * t, 0:TH], ACT.Silu).then_inc(silu_ready, 1)

            def act_high(u, r, ring_free=None):
                act.wait_ge(act_ready, u + 1)
                if ring_free is not None:
                    act.wait_ge(down_done, ring_free)
                nc.scalar.copy(ahi[:, r, :], ac[:, r, :]).then_inc(ahi_ready, 1)

            split_high(3, 3)
            silu(0, 0)
            silu(1, 0, 1)
            act_high(0, 0)
            squares(1, 1)
            act_high(1, 1)
            silu(2, 0, 2)
            load_table(2, ACT.Sqrt)
            root(1, 1, 7)
            load_table(3, ACT.Sigmoid)
            split_x(1)
            act.wait_ge(logit_done, 2)
            nc.scalar.activation(g_s[:, :, :].rearrange("p t e -> p (t e)"), ps[0:PAIR, 7, 0:NT * E],
                                 ACT.Sigmoid).then_inc(sig_ready, 1)
            silu(3, 0, 3)
            silu(4, 1)
            silu(5, 1, 5)
            act_high(2, 2)
            silu(6, 1, 6)
            act_high(3, 3)
            act.wait_ge(combT_done, 1)
            for i in range(2):
                nc.scalar.copy(cT[:, half(i)], ps[0:E, i, 0:TH]).then_inc(combT_ready, 1)
            split_high(RING, 0, 4)
            silu(7, 1, 7)
            for t in range(2):
                act_high(2 * NSH + t, t, t + 1)

            def expert(n, slot, last):
                if not last:
                    split_high(n + 1, (slot + 1) % RING, 2 * (n + 1 - RING) + 2)
                for t in range(2):
                    u = 2 * n + t
                    silu(u, t, u - 1)
                    act_high(u - 2, (2 * slot + 2 + t) % RING, u - 2 - RING + 1)

            with act.Fori(0, (NE - 2 - RING) // RING) as turn_of_ring:
                n0 = turn_of_ring * RING + RING
                for k in range(RING):
                    expert(n0 + k, k, False)
            for n in range(NE - 2, NE):
                expert(n, n % RING, n == NE - 1)
            for t in range(2):
                u = 2 * (NE - 1) + t
                act_high(u, u % RING, u - RING + 1)

        @block.gpsimd
        def _(pool):
            nc.gpsimd.memset(zb[:, :, :, L:ZW], NEG).then_inc(zmask_ready, 1)
            pool.wait_ge(cst_in, 16)
            for s in range(MC):
                nc.gpsimd.tensor_copy(ke[:, s, :, L:PAIR],
                                      col(C_REL, L).unsqueeze(1).broadcast_to([128, B, L])).then_inc(ke_rel, 1)
            nc.gpsimd.memset(yb[:, :, :, :], 0.0).then_inc(y_zero, 1)
            pool.wait_ge(proj_done, 2 * MC)
            nc.gpsimd.memset(qbd[:, :, :, 8 * L:IW], 0.0).then_inc(qbd_zero, 1)

            def cosine(t):
                pool.wait_ge(qk_ready, 2 * t + 2)
                if t == 1:
                    pool.wait_ge(krot_ready, 1)
                nc.gpsimd.tensor_tensor(
                    qkc[:, :, :, :].rearrange("p a s (b n) -> p (a s b) n", n=L),
                    qk[:, :, :, :].rearrange("p a s (b n) -> p (a s b) n", n=L),
                    col(C_COS, L).unsqueeze(1).broadcast_to([128, 4 * HB, L]), ALU.mult).then_inc(cos_ready, 1)

            cosine(0)
            for t in range(2):
                pool.wait_ge(rs_ready, t + 1)
                nc.gpsimd.tensor_tensor(xn[:, :, half(t)], dT[:, :, half(t)],
                                        rs[:, half(t)].unsqueeze(1).broadcast_to([128, MC, TH]),
                                        ALU.mult).then_inc(xn_ready, 1)
                if t == 1:
                    cosine(1)

            pool.wait_ge(y_zero, 1)
            for st in range(NSTEP):
                pool.wait_ge(inv_ready, st + 1)
                if st >= DEPTH:
                    pool.wait_ge(tr_done, IPS * (st - DEPTH + 1))
                nc.gpsimd.tensor_tensor(yb[:, st % DEPTH, :, L - 1:2 * L - 1], sc[:, st % DEPTH, :, :],
                                        st_inv[:, st % DEPTH, :].unsqueeze(2).broadcast_to([HR, CH, L]),
                                        ALU.mult).then_inc(prob_ready, 1)

            pool.wait_ge(wo_done, 2 * MC)
            for n in range(NSH):
                nc.gpsimd.memset(cb[:, n, :], 1.0).then_inc(ones_ready, 1)
            pool.wait_ge(ones_ready, NSH)

            def weigh(u, r, slot, t, ring_free=None, made=None):
                made = u if made is None else made
                pool.wait_ge(gu_ready, made + 1)
                if ring_free is not None:
                    pool.wait_ge(ahi_ready, ring_free)
                    pool.wait_ge(alo_ready, ring_free)
                nc.gpsimd.tensor_tensor(ac[:, r, :], gu[:, r if type(made) is not int else made % RING, :], cb[:, slot, half(t)],
                                        ALU.mult).then_inc(act_ready, 1)

            for u in range(2 * NSH):
                weigh(u, u, u % NSH, u // NSH, made=u % NSH + RING * (u // NSH))
            for n in range(NSH, RING):
                pool.wait_ge(cb_in[n], 16)
                for t in range(2):
                    u = 2 * n + t
                    weigh(u, u % RING, n, t, u - RING + 1, made=n + RING * t)
            with pool.Fori(0, (NE - 2 - RING) // RING) as turn_of_ring:
                n0 = turn_of_ring * RING + RING
                for k in range(RING):
                    pool.wait_ge(cb_in[k], 4 * n0 if k < NSH else 4 * n0 + 16)
                    for t in range(2):
                        u = 2 * (n0 + k) + t
                        weigh(u, (2 * k + t) % RING, k, t, u - RING + 1)
            for n in range(NE - 2, NE):
                pool.wait_ge(cb_in[n % RING], 16 * (n // RING))
                for t in range(2):
                    u = 2 * n + t
                    weigh(u, u % RING, n % RING, t, u - RING + 1)


def tables():
    inv = (1.0 / np.float32(10000.0) ** (np.arange(0, HD, 2, dtype=np.float32) / np.float32(HD))).astype(np.float32)
    ang = np.outer(np.arange(L, dtype=np.float32), inv).astype(np.float32)
    f = (np.arange(128) % HD) // 2
    cos = np.cos(ang)[:, f].T.astype(np.float32)
    sin = np.sin(ang)[:, f].T.astype(np.float32)
    sin = np.where((np.arange(128) % 2 == 0)[:, None], -sin, sin)
    first = (np.arange(128) % 32 < HD).astype(np.float32)
    pair = np.stack([first, 1 - first], 1)
    low = np.broadcast_to((np.arange(G)[None, :] < np.arange(G)[:, None]).astype(np.float32).reshape(1, G * G),
                          (128, G * G))
    heads = (np.arange(128)[:, None] // HD == np.arange(128 // HD)[None, :]).astype(np.float32)
    return cos, sin, heads * np.float32(0.25), pair, low


def kernel(x, L0_tok_W, L0_tok_b, L0_tok_class_token, L0_tok_pos_embedding, L0_attn_w_q, L0_attn_w_k, L0_attn_w_v,
           L0_attn_w_o, L0_attn_rel_emb, L0_ffn_gate_w, L0_ffn_gate_bias, L0_ffn_w_gate, L0_ffn_w_up, L0_ffn_w_down,
           L0_ffn_sh_gate, L0_ffn_sh_up, L0_ffn_sh_down):
    import concourse.bacc as bacc
    from concourse.bass_utils import run_bass_kernel_spmd

    a = np.asarray
    P = 16
    pat = a(x).reshape(B, 3, 6, P, 6, P).transpose(1, 3, 5, 0, 2, 4).reshape(KP, 128, B * NP)
    wtok = a(L0_tok_W).T.reshape(KP, 128, D)
    emb = np.ascontiguousarray(np.concatenate([wtok, pat], axis=2))
    offs = np.clip(np.arange(L) - (L - 1), -32, 32) + 32
    rel = a(L0_attn_rel_emb)[offs]
    rel_v = np.ascontiguousarray(np.tile(rel, (1, D // HD)))
    cos, sin, heads, pair, low = tables()

    def cols(v):
        return v.reshape(-1, MC, 128).transpose(2, 1, 0).reshape(128, -1)

    const = np.ascontiguousarray(np.concatenate([
        cols(a(L0_tok_b)), cols(a(L0_tok_class_token)), cols(a(L0_tok_pos_embedding)[0]), cos, sin,
        heads, pair, np.tile(rel.T, (128 // HD, 1)), cols(a(L0_ffn_gate_w)),
        np.broadcast_to(a(L0_ffn_gate_bias), (128, E)), low, np.full((128, 1), EPS), np.full((128, 128), 1 / D),
        np.eye(128)], axis=1), dtype=np.float32)
    wattn = np.ascontiguousarray(np.stack([a(w).T.reshape(MC, 128, D).transpose(1, 0, 2) for w in
                                           (L0_attn_w_q, L0_attn_w_k, L0_attn_w_v, L0_attn_w_o)], axis=1))

    def side(w):
        return w.reshape(-1, INTER, MC, 128).transpose(0, 3, 2, 1).reshape(-1, 128, D)

    wexp = np.ascontiguousarray(np.concatenate([
        np.concatenate([side(a(L0_ffn_sh_gate)), side(a(L0_ffn_w_gate))]),
        np.concatenate([side(a(L0_ffn_sh_up)), side(a(L0_ffn_w_up))]),
        np.concatenate([a(L0_ffn_sh_down).reshape(D, NSH, INTER).transpose(1, 2, 0),
                        a(L0_ffn_w_down).transpose(0, 2, 1)])], axis=2))

    nc = bacc.Bacc("TRN2", target_bir_lowering=False, num_devices=1)
    arrays = {"emb": emb, "cst": const, "rel_v": rel_v, "wattn": wattn, "wexp": wexp}
    aps = [nc.dram_tensor(n, v.shape, F32, kind="ExternalInput").ap() for n, v in arrays.items()]
    aps.append(nc.dram_tensor("out", (MC, 128, T), F32, kind="ExternalOutput").ap())
    build(nc, *aps)
    r = run_bass_kernel_spmd(nc, [arrays], core_ids=[0])
    return np.ascontiguousarray(r.results[0]["out"].reshape(MC, 128, B, L).transpose(2, 3, 0, 1).reshape(B, L, D))
```

```python
from contextlib import ExitStack

import numpy as np

import concourse.bass as bass
from concourse import mybir

F32 = mybir.dt.float32
F32R = mybir.dt.float32r
ALU = mybir.AluOpType
ACT = mybir.ActivationFunctionType
AX_X = mybir.AxisListType.X

B, L, D = 16, 37, 256
NP = L - 1
T = B * L
KP = 768 // 128
MC = D // 128
HB = B // 2
TH = HB * L
TP = HB * NP
HD = 16
E, INTER = 32, 128
NSH = 2
G, GE, TKG, TOPK = 8, 4, 4, 8
SCALE = 2.5
NEG = -1e18
EPS = 1e-5

IPS = 4
SPH = MC * HB // IPS
NSTEP = 2 * SPH
HPM = 3
MPI = 3
HR = HPM * L
CH = MPI * IPS
PAIR = 2 * L
IW = MPI * HR
DEPTH = 4
LEAD = DEPTH + 1
LAG = 2
WARM_UP, FILL, TAIL_FILL = 4, 10, 4
ZW = 2 * L - 1
YW = 3 * L - 1
ROW = CH * YW + L
STEP = HR * (ROW + 1)

NE = NSH + E
QD = 5
RING = 4
WE = 3 * 2 * 128

C_BIAS = 0
C_CLS = C_BIAS + MC
C_POS = C_CLS + MC
C_COS = C_POS + MC * L
C_SIN = C_COS + L
C_QM = C_SIN + L
C_OM = C_QM + 8
C_REL = C_OM + 2
C_GW = C_REL + L
C_GB = C_GW + MC * E
C_EPS = C_GB + E
C_ONE = C_EPS + 1
C_ID = C_ONE + 128
C_ALL = C_ID + 128


def build(nc, emb, cst, rel_v, wattn, wexp, out):
    zd = nc.dram_tensor("rel_scores", (NSTEP, STEP), F32)
    yd = nc.dram_tensor("probs", (NSTEP, STEP), F32)
    cd = nc.dram_tensor("combine", (E, T), F32).ap()

    with ExitStack() as ctx:
        def sem(name):
            return ctx.enter_context(nc.semaphore(name))

        def sb(name, shape, dt=F32, scope=ctx):
            return scope.enter_context(nc.sbuf_tensor(name, shape, dt))

        ps = ctx.enter_context(nc.psum_tensor("ps", [128, 8, 512], F32))

        cs = sb("cs", [128, C_ALL])
        hT = sb("hT", [128, MC, T])
        dT = sb("dT", [128, MC, T])
        sd = sb("sd", [128, T])
        rs = sb("rs", [128, T])
        warm = sb("warm", [128, 4])
        idle = sb("idle", [128, 256])
        xn = sb("xn", [128, MC, T])
        wst = sb("wst", [128, RING, WE])
        whi = sb("whi", [128, RING, WE], F32R)
        wlo = sb("wlo", [128, RING, WE], F32R)
        xhi = sb("xhi", [128, MC, T], F32R)
        xlo = sb("xlo", [128, MC, T], F32R)

        attn = ExitStack()
        wat = sb("wat", [128, 4, MC, D], F32, attn)
        qk = sb("qk", [128, 2, MC, TH], F32, attn)
        qksw = sb("qksw", [128, 2, MC, TH], F32, attn)
        qkc = sb("qkc", [128, 2, MC, TH], F32, attn)
        qrot = sb("qrot", [128, MC, TH], F32, attn)
        ke = sb("ke", [128, MC, B, PAIR], F32, attn)
        ve = sb("ve", [PAIR, B, D], F32, attn)
        zb = sb("zb", [HR, DEPTH, CH, ZW], F32, attn)
        sc = sb("sc", [HR, DEPTH, CH, L], F32, attn)
        rl = sb("rl", [HR, DEPTH, CH, L], F32, attn)
        st_mx = sb("st_mx", [HR, CH], F32, attn)
        st_sum = sb("st_sum", [HR, 2, CH], F32, attn)
        st_inv = sb("st_inv", [HR, DEPTH, CH], F32, attn)
        cth = sb("cth", [128, 2, IPS, L], F32, attn)
        ctxT = sb("ctxT", [128, MC, T], F32, attn)
        first = ExitStack()
        vt = sb("vt", [HR, 6, D], F32, first)
        first.close()
        pt = sb("pt", [PAIR, 2, IPS, IW], F32, attn)
        first = ExitStack()
        em = sb("em", [128, KP, D + 2 * TP], F32, first)
        first.close()
        qbd = sb("qbd", [128, MC, HB, IW], F32, attn)
        yb = sb("yb", [HR, DEPTH, CH, YW], F32, attn)
        attn.close()

        cb = sb("cb", [128, RING, T])
        sg = sb("sg", [128, 2, TH])
        gu = sb("gu", [128, RING, TH])
        ac = sb("ac", [128, RING, TH])
        ahi = sb("ahi", [128, RING, TH], F32R)
        alo = sb("alo", [128, RING, TH], F32R)
        oT = sb("oT", [128, MC, T])
        cT = sb("cT", [E, T])
        NT = T // PAIR
        g_s = sb("g_s", [PAIR, NT, E])
        g_sc = sb("g_sc", [PAIR, NT, E])
        g_pair = sb("g_pair", [PAIR, NT * G, 6])
        g_gs = sb("g_gs", [PAIR, NT, G])
        g_gtop = sb("g_gtop", [PAIR, NT, G])
        g_grep = sb("g_grep", [PAIR, NT, G])
        g_gm = sb("g_gm", [PAIR, NT * G])
        g_mk = sb("g_mk", [PAIR, NT, E])
        g_top = sb("g_top", [PAIR, NT, TOPK])
        g_rep = sb("g_rep", [PAIR, NT, E])
        g_sel = sb("g_sel", [PAIR, NT, E])
        g_w = sb("g_w", [PAIR, NT, E])
        g_sum = sb("g_sum", [PAIR, NT])
        g_inv = sb("g_inv", [PAIR, NT])
        g_cw = sb("g_cw", [PAIR, NT, E])

        em_in = [sem(f"em_in{c}") for c in range(KP)]
        em2_in = [sem(f"em2_in{c}") for c in range(KP)]
        wat_in = [sem(f"wat_in{m}") for m in range(4)]
        cst_in, relv_in, v_moved = sem("cst_in"), sem("relv_in"), sem("v_moved")
        wt_in = [sem(f"wt_in{s}") for s in range(RING)]
        cb_in = [sem(f"cb_in{s}") for s in range(RING)]
        z_out = [sem(f"z_out{g}") for g in range(NSTEP)]
        z_in = [sem(f"z_in{g}") for g in range(NSTEP)]
        y_out = [sem(f"y_out{g}") for g in range(NSTEP)]
        y_in = [sem(f"y_in{g}") for g in range(NSTEP)]
        comb_out, out_done = sem("comb_out"), sem("out_done")
        proj_done, h_ready = sem("proj_done"), sem("h_ready")
        mean_done, d_ready, sq_ready, var_done = sem("mean_done"), sem("d_ready"), sem("sq_ready"), sem("var_done")
        sd_ready, rs_ready, xn_ready = sem("sd_ready"), sem("rs_ready"), sem("xn_ready")
        qk_done, qk_ready = sem("qk_done"), sem("qk_ready")
        v_done, v_copied = sem("v_done"), sem("v_copied")
        shuf_ready, sin_ready, cos_ready = sem("shuf_ready"), sem("sin_ready"), sem("cos_ready")
        qrot_ready, krot_ready = sem("qrot_ready"), sem("krot_ready")
        qbd_dve, qbd_act, qbd_zero = sem("qbd_dve"), sem("qbd_act"), sem("qbd_zero")
        ke_rel, zmask_ready, y_zero = sem("ke_rel"), sem("zmask_ready"), sem("y_zero")
        score_done, score_copied = sem("score_done"), sem("score_copied")
        sum_ready, max_ready, shift_ready = sem("sum_ready"), sem("max_ready"), sem("shift_ready")
        exp_ready, den_ready = sem("exp_ready"), sem("den_ready")
        inv_ready, prob_ready = sem("inv_ready"), sem("prob_ready")
        tr_done, pt_even, pt_odd = sem("tr_done"), sem("pt_even"), sem("pt_odd")
        ctx_done, ctx_half, ctx_ready = sem("ctx_done"), sem("ctx_half"), sem("ctx_ready")
        wo_done, h2_ready = sem("wo_done"), sem("h2_ready")
        xhi_ready, xlo_ready = sem("xhi_ready"), sem("xlo_ready")
        logit_done, sig_ready, route, comb_ready = sem("logit_done"), sem("sig_ready"), sem("route"), sem("comb_ready")
        combT_done, combT_ready = sem("combT_done"), sem("combT_ready")
        row_done, row_ready = sem("row_done"), sem("row_ready")
        ones_ready, warm_done, idle_ready = sem("ones_ready"), sem("warm_done"), sem("idle_ready")
        whi_ready, wlo_ready = sem("whi_ready"), sem("wlo_ready")
        gate_done, up_done, down_done = sem("gate_done"), sem("up_done"), sem("down_done")
        silu_ready, gu_ready, act_ready = sem("silu_ready"), sem("gu_ready"), sem("act_ready")
        ahi_ready, alo_ready, out_ready = sem("ahi_ready"), sem("alo_ready"), sem("out_ready")

        def half(t):
            return slice(t * TH, (t + 1) * TH)

        def col(a, n):
            return cs[:, a:a + n]

        ident = cs[:, C_ID:C_ID + 128]
        mean_w = cs[:, C_ONE:C_ONE + 128]
        hv = hT[:, :, :].rearrange("p m (b n) -> p m b n", n=L)

        def where(st):
            t, s, q = st // SPH, (st % SPH) // (HB // IPS), st % (HB // IPS)
            return t, s, t * HB + q * IPS

        QK_BANKS = ((4, 2), (6, 0))

        def score_banks(st):
            return 4 + 2 * (st % 2)

        def rows(dram, width, shift, st):
            return bass.AP(dram, st * STEP, [[L * (ROW + shift), HPM], [ROW, L], [1, CH * width]])

        def shifted_rows(dram, width, shift, st, start):
            return bass.AP(dram, st * STEP + start, [[ROW + shift, HR], [width, CH], [1, L]])

        block = ctx.enter_context(nc.Block())

        @block.sync
        def _(sp):
            for c in range(0, KP, 2):
                sp.dma_start(em[:, c, 0:D + TP], emb[c][:, 0:D + TP]).then_inc(em_in[c], 16)
            sp.dma_start(wat[:, 0, :, :], wattn[:, 0, :, :]).then_inc(wat_in[0], 16)
            for c in range(0, KP, 2):
                sp.dma_start(em[:, c, D + TP:D + 2 * TP], emb[c][:, D + TP:D + 2 * TP]).then_inc(em2_in[c], 16)
            for mat in range(1, 4):
                sp.dma_start(wat[:, mat, :, :], wattn[:, mat, :, :]).then_inc(wat_in[mat], 16)
            for n in range(RING):
                sp.dma_start(wst[:, n, :], wexp[n]).then_inc(wt_in[n], 16)

            def scores_in(st):
                sp.wait_ge(z_out[st], 16)
                if st >= DEPTH:
                    sp.wait_ge(sum_ready, st - DEPTH + 1)
                sp.dma_start(rl[:, st % DEPTH, :, :], shifted_rows(zd, ZW, -1, st, L - 1)).then_inc(z_in[st], 16)

            def probs_out(st):
                sp.wait_ge(prob_ready, st + 1)
                sp.dma_start(rows(yd, YW, 1, st),
                             yb[:, st % DEPTH, :, :].rearrange("p c k -> p (c k)")).then_inc(y_out[st], 16)

            def probs_in(st):
                sp.wait_ge(y_out[st], 16)
                sp.dma_start(yb[:, st % DEPTH, :, YW - L:YW], shifted_rows(yd, YW, 1, st, 0)).then_inc(y_in[st], 16)

            for st in range(2):
                scores_in(st)
            sp.wait_ge(v_copied, 6)
            for r in range(3):
                n = (B - r + 2) // 3
                sp.dma_start(ve[0:L, r:B:3, :], vt[r * L:(r + 1) * L, 0:n, :]).then_inc(v_moved, 16)
            probs_out(0)
            scores_in(2)
            probs_in(0)
            probs_out(1)
            for st in range(DEPTH - 1, LEAD):
                scores_in(st)
            probs_in(1)
            probs_out(2)
            probs_in(2)
            for st in range(LEAD, NSTEP):
                probs_out(st - LAG)
                scores_in(st)
                probs_in(st - LAG)
            for st in range(NSTEP - LAG, NSTEP):
                probs_out(st)
                probs_in(st)

            def weights(n, slot):
                sp.wait_ge(whi_ready, n - RING + 1)
                sp.wait_ge(wlo_ready, n - RING + 1)
                sp.dma_start(wst[:, slot, :], wexp[n] if type(n) is int else
                             wexp[bass.ds(n, 1)].rearrange("o p w -> (o p) w")).then_inc(wt_in[slot], 16)

            def combine(n, slot):
                sp.wait_ge(act_ready, 2 * (n - RING) + 3)
                row = cd[n - NSH:n - NSH + 1, :] if type(n) is int else cd[bass.ds(n - NSH, 1), :]
                sp.dma_start(cb[:, slot, :], row.broadcast_to([128, T])).then_inc(cb_in[slot], 16)

            for n in range(RING, RING + 2):
                weights(n, n - RING)
            sp.wait_ge(combT_ready, 2)
            sp.dma_start(cd, cT[:, :]).then_inc(comb_out, 16)
            sp.wait_ge(comb_out, 16)

            for n in range(NSH + 1, RING):
                sp.dma_start(cb[:, n, :], cd[n - NSH:n - NSH + 1, :].broadcast_to([128, T])).then_inc(cb_in[n], 16)
            with sp.Fori(0, (NE - 2 - RING) // RING) as turn_of_ring:
                n0 = turn_of_ring * RING + RING
                for k in range(RING):
                    combine(n0 + k, k)
                    weights(n0 + k + 2, (k + 2) % RING)
            combine(NE - 2, (NE - 2) % RING)
            combine(NE - 1, (NE - 1) % RING)
            for t in range(2):
                sp.wait_ge(out_ready, MC * (t + 1))
                sp.dma_start(out.rearrange("m p t -> p m t")[:, :, half(t)], oT[:, :, half(t)]).then_inc(out_done, 16)
            sp.wait_ge(out_done, 32)

        @block.tensor
        def _(pe):
            def mean(t, bank):
                for m in range(MC):
                    mm = nc.tensor.matmul(ps[:, bank, 0:TH], mean_w, hT[:, m, half(t)],
                                          start=(m == 0), stop=(m == MC - 1))
                mm.then_inc(mean_done, 1)

            def variance(k, t, bank):
                pe.wait_ge(sq_ready, 2 * k + t + 1)
                for m in range(MC):
                    mm = nc.tensor.matmul(ps[:, bank, 0:TH], mean_w, xn[:, m, half(t)],
                                          start=(m == 0), stop=(m == MC - 1))
                mm.then_inc(var_done, 1)

            def query_key(t, mat):
                bank = QK_BANKS[t][mat]
                for s in range(MC):
                    for m in range(MC):
                        mm = nc.tensor.matmul(ps[:, bank + s, 0:TH],
                                              wat[:, mat, m, s * 128:(s + 1) * 128], dT[:, m, half(t)],
                                              start=(m == 0), stop=(m == MC - 1))
                mm.then_inc(qk_done, 1)

            def keep_clock(count, bank):
                for _ in range(count):
                    nc.tensor.matmul(ps[:, bank, 0:256], idle[:, 0:128], idle[:, :], start=True, stop=True)

            def embed(t, arrived, chunks):
                for c in chunks:
                    pe.wait_ge(arrived[c], 16)
                    for m in range(MC):
                        mm = nc.tensor.matmul(ps[:, 4 + 2 * t + m, 0:TP], em[:, c, m * 128:(m + 1) * 128],
                                              em[:, c, D + t * TP:D + (t + 1) * TP],
                                              start=(c == 0), stop=(c == KP - 1))
                        if c == KP - 1:
                            mm.then_inc(proj_done, 1)

            pe.wait_ge(idle_ready, 1)
            keep_clock(WARM_UP, 0)
            embed(0, em_in, range(KP))
            embed(1, em2_in, range(0, 1))
            pe.wait_ge(cst_in, 16)
            pe.wait_ge(h_ready, 2 * MC)
            mean(0, 0)
            embed(1, em2_in, range(1, 3))
            pe.wait_ge(d_ready, 1)
            variance(0, 0, 0)
            pe.wait_ge(wat_in[0], 16)
            query_key(0, 0)
            pe.wait_ge(wat_in[1], 16)
            query_key(0, 1)
            embed(1, em2_in, range(3, KP))
            pe.wait_ge(h_ready, 3 * MC)
            mean(1, 1)
            pe.wait_ge(d_ready, 2)
            query_key(1, 0)
            variance(0, 1, 1)

            def values():
                pe.wait_ge(wat_in[2], 16)
                pe.wait_ge(xn_ready, 2)
                pe.wait_ge(qk_ready, 4)
                for i in range(6):
                    n = min(HR, T - i * HR)
                    for m in range(MC):
                        mm = nc.tensor.matmul(ps[0:n, i // 2, (i % 2) * D:(i % 2 + 1) * D],
                                              xn[:, m, i * HR:i * HR + n], wat[:, 2, m, :],
                                              start=(m == 0), stop=(m == MC - 1))
                    if i % 2:
                        mm.then_inc(v_done, 1)

            def scores_wait(st):
                t, s, b0 = where(st)
                if st == 0:
                    pe.wait_ge(ke_rel, MC)
                    pe.wait_ge(qk_ready, 1)
                    pe.wait_ge(qbd_zero, 1)
                if st == 1:
                    pe.wait_ge(qk_ready, 3)
                if st % SPH == 0:
                    pe.wait_ge(krot_ready, t + 1)
                if st % (HB // IPS) == 0:
                    pe.wait_ge(qbd_dve, QD * (MC * t + s + 1))
                    pe.wait_ge(qbd_act, (8 - QD) * (MC * t + s + 1))
                if st >= 2:
                    pe.wait_ge(score_copied, 2 * (st - 1))

            def scores_image(st, i):
                t, s, b0 = where(st)
                for m in range(MPI):
                    c = i * MPI + m
                    mm = nc.tensor.matmul(
                        ps[0:HR, score_banks(st) + c // 6, (c % 6) * PAIR:(c % 6 + 1) * PAIR],
                        qbd[:, s, b0 % HB + i, m * HR:(m + 1) * HR], ke[:, s, b0 + i, :],
                        start=True, stop=True)
                if i == IPS - 1:
                    mm.then_inc(score_done, 1)

            def turn_wait(st):
                pe.wait_ge(y_in[st], 16)
                if st == 0:
                    pe.wait_ge(v_copied, 6)

            def turn_image(st, i):
                u = st * IPS + i
                if u >= 2:
                    pe.wait_ge(pt_odd if u % 2 else pt_even, u // 2)
                for m in range(MPI):
                    mm = nc.tensor.transpose(ps[0:PAIR, u % 2, m * HR:(m + 1) * HR],
                                             yb[:, st % DEPTH, i * MPI + m, L - 1:YW], ident[0:HR, 0:HR])
                mm.then_inc(tr_done, 1)

            def context_wait(st):
                pe.wait_ge(pt_even, 2 * (st + 1))
                pe.wait_ge(pt_odd, 2 * (st + 1))
                if st == 0:
                    pe.wait_ge(relv_in, 16)
                    pe.wait_ge(v_moved, 3 * 16)
                if st >= 2:
                    pe.wait_ge(ctx_ready, st - 1)

            def context_image(st, i):
                t, s, b0 = where(st)
                for j in range(4):
                    mm = nc.tensor.matmul(ps[32 * j:32 * j + 32, 2 + st % 2, i * PAIR:(i + 1) * PAIR],
                                          ve[:, b0 + i, s * 128 + 32 * j:s * 128 + 32 * j + 32],
                                          pt[:, st % 2, i, j * PAIR:(j + 1) * PAIR], start=True, stop=True)
                if i == IPS - 1:
                    mm.then_inc(ctx_done, 1)

            def project(t, bank):
                pe.wait_ge(ctx_ready, SPH * (t + 1))
                pe.wait_ge(wat_in[3], 16)
                for m in range(MC):
                    for s in range(MC):
                        mm = nc.tensor.matmul(ps[:, bank + m, 0:TH], wat[:, 3, s, m * 128:(m + 1) * 128],
                                              ctxT[:, s, half(t)], start=(s == 0), stop=(s == MC - 1))
                    mm.then_inc(wo_done, 1)

            for st in range(LEAD):
                scores_wait(st)
                for k in range(IPS):
                    scores_image(st, k)
                if st == 0:
                    pe.wait_ge(sd_ready, 2)
                    query_key(1, 1)
                if st == 1:
                    values()
            keep_clock(FILL, 3)
            for st in range(LEAD, NSTEP):
                scores_wait(st)
                if st == LEAD + 1:
                    keep_clock(TAIL_FILL + 1, score_banks(st) + 1)
                turn_wait(st - LEAD)
                if st > LEAD:
                    context_wait(st - LEAD - 1)
                for k in range(IPS):
                    turn_image(st - LEAD, k)
                    scores_image(st, k)
                    if st > LEAD:
                        context_image(st - LEAD - 1, k)
            for st in range(NSTEP - LEAD, NSTEP + 1):
                context_wait(st - 1)
                for k in range(IPS):
                    context_image(st - 1, k)
                if st < NSTEP:
                    if st == SPH:
                        pe.wait_ge(score_copied, 2 * NSTEP)
                    turn_wait(st)
                    for k in range(IPS):
                        turn_image(st, k)
                        if st == NSTEP - 1 and k == 1:
                            keep_clock(1, 5)
                if st == SPH:
                    project(0, 4)
                if st == SPH + 1:
                    keep_clock(TAIL_FILL // 2, 7)
                    pe.wait_ge(h2_ready, MC)
                    mean(0, 6)
                if st == SPH + 2:
                    variance(1, 0, 7)

            def gate_up(n, slot, t, pair, pair_free):
                if t == 0:
                    pe.wait_ge(whi_ready, n + 1)
                    pe.wait_ge(wlo_ready, n + 1)
                if pair_free is not None:
                    pe.wait_ge(gu_ready, pair_free)
                for mat, done in ((0, gate_done), (1, up_done)):
                    k = 0
                    for m in range(MC):
                        a = (2 * mat + m) * 128
                        for w, x in ((whi, xhi), (whi, xlo), (wlo, xhi)):
                            mm = nc.tensor.matmul(ps[:, 2 * pair + mat, 0:TH], w[:, slot, a:a + 128],
                                                  x[:, m, half(t)], start=(k == 0), stop=(k == 3 * MC - 1))
                            k += 1
                    mm.then_inc(done, 1)

            def down(u, slot, r, t, start=False, stop=False):
                pe.wait_ge(ahi_ready, u + 1)
                pe.wait_ge(alo_ready, u + 1)
                for m in range(MC):
                    a = (4 + m) * 128
                    for k, (w, x) in enumerate(((whi, ahi), (whi, alo), (wlo, ahi))):
                        mm = nc.tensor.matmul(ps[:, 4 + 2 * t + m, 0:TH], w[:, slot, a:a + 128], x[:, r, :],
                                              start=(start and k == 0), stop=(stop and k == 2),
                                              skip_group_check=True)
                mm.then_inc(down_done, 1)

            def logits(t):
                pe.wait_ge(xn_ready, 2 + t + 1)
                for i in range(NT // 2 * t, NT // 2 * (t + 1)):
                    for m in range(MC):
                        mm = nc.tensor.matmul(ps[0:PAIR, 6, i * E:(i + 1) * E], xn[:, m, i * PAIR:(i + 1) * PAIR],
                                              cs[:, C_GW + m * E:C_GW + (m + 1) * E],
                                              start=(m == 0), stop=(m == MC - 1))
                mm.then_inc(logit_done, 1)

            keep_clock(2, 5)
            project(1, 2)
            pe.wait_ge(h2_ready, 2 * MC)
            pe.wait_ge(d_ready, 3)
            mean(1, 6)
            pe.wait_ge(xhi_ready, 1)
            pe.wait_ge(xlo_ready, 1)
            gate_up(0, 0, 0, 0, None)
            pe.wait_ge(sd_ready, 3)
            variance(1, 1, 7)
            gate_up(1, 1, 0, 1, None)
            pe.wait_ge(d_ready, 4)
            logits(0)
            keep_clock(TAIL_FILL // 2, 4)
            logits(1)
            gate_up(2, 2, 0, 0, 1)
            gate_up(3, 3, 0, 1, 2)
            down(0, 0, 0, 0, start=True)
            down(1, 1, 1, 0)
            pe.wait_ge(xhi_ready, 2)
            pe.wait_ge(xlo_ready, 2)
            gate_up(0, 0, 1, 0, 3)
            gate_up(1, 1, 1, 1, 4)
            gate_up(2, 2, 1, 0, 5)
            pe.wait_ge(sig_ready, 1)
            down(2, 0, 2, 1, start=True)
            pe.wait_ge(gu_ready, 6)
            keep_clock(1, 2)
            pe.wait_ge(comb_ready, 1)
            for i in range(NT):
                mm = nc.tensor.transpose(ps[0:E, 2 + i // 4, (i % 4) * PAIR:(i % 4 + 1) * PAIR], g_cw[:, i, :],
                                         ident[0:PAIR, 0:PAIR])
            mm.then_inc(combT_done, 1)
            down(3, 1, 3, 1)
            pe.wait_ge(combT_ready, 2)
            pe.wait_ge(gu_ready, 7)
            for t in range(2):
                mm = nc.tensor.matmul(ps[:, t, 0:TH], ident[0:E, 0:1].broadcast_to([E, 128]), cT[:, half(t)],
                                      start=True, stop=True)
            mm.then_inc(row_done, 1)
            gate_up(3, 3, 1, 1, None)
            pe.wait_ge(row_ready, 1)

            def expert(n, slot):
                for t in range(2):
                    gate_up(n, slot, t, t, 2 * n + t - 1)
                    down(2 * (n - 2) + t, (slot - 2) % RING, (2 * slot + t) % RING, t)

            with pe.Fori(0, (NE - 2 - RING) // RING) as turn_of_ring:
                n0 = turn_of_ring * RING + RING
                for k in range(RING):
                    expert(n0 + k, k)
            for n in range(NE - 2, NE):
                expert(n, n % RING)
            for n in range(NE - 2, NE):
                for t in range(2):
                    down(2 * n + t, n % RING, (2 * n + t) % RING, t, stop=(n == NE - 1))

        @block.vector
        def _(dve):
            nc.vector.memset(idle[:, :], 0.0).then_inc(idle_ready, 1)
            dve.wait_ge(cst_in, 16)
            for m in range(MC):
                nc.vector.tensor_tensor(hv[:, m, :, 0], col(C_CLS + m, 1).broadcast_to([128, B]),
                                        col(C_POS + m * L, 1).broadcast_to([128, B]), ALU.add).then_inc(h_ready, 1)

            def centre(k, t, bank):
                dve.wait_ge(mean_done, 2 * k + t + 1)
                nc.vector.tensor_tensor(dT[:, :, half(t)], hT[:, :, half(t)],
                                        ps[:, bank, 0:TH].unsqueeze(1).broadcast_to([128, MC, TH]),
                                        ALU.subtract).then_inc(d_ready, 1)

            def deviation(k, t):
                dve.wait_ge(sd_ready, 2 * k + t + 1)
                nc.vector.reciprocal(rs[:, half(t)], sd[:, half(t)]).then_inc(rs_ready, 1)
                dve.wait_ge(rs_ready, 2 * k + t + 1)

            def embed(t):
                for m in range(MC):
                    dve.wait_ge(proj_done, 2 * t + m + 1)
                    nc.vector.scalar_tensor_tensor(
                        out=hv[:, m, t * HB:(t + 1) * HB, 1:L],
                        in0=ps[:, 4 + 2 * t + m, 0:TP].rearrange("p (b n) -> p b n", n=NP),
                        scalar=col(C_BIAS + m, 1),
                        in1=cs[:, C_POS + m * L + 1:C_POS + (m + 1) * L].unsqueeze(1).broadcast_to([128, HB, NP]),
                        op0=ALU.add, op1=ALU.add).then_inc(h_ready, 1)

            embed(0)
            centre(0, 0, 0)

            swap = [i ^ 1 for i in range(32)]

            def divide(t):
                deviation(0, t)
                if t == 1:
                    dve.wait_ge(cos_ready, 1)
                for mat in range(2):
                    dve.wait_ge(qk_done, 2 * t + mat + 1)
                    nc.vector.tensor_tensor(qk[:, mat, :, :], ps[:, QK_BANKS[t][mat]:QK_BANKS[t][mat] + 2, 0:TH],
                                            rs[:, half(t)].unsqueeze(1).broadcast_to([128, MC, TH]),
                                            ALU.mult).then_inc(qk_ready, 1)

            def shuffle(t):
                dve.wait_ge(qk_ready, 2 * t + 2)
                nc.vector.stream_shuffle(qksw[:, :, :, :], qk[:, :, :, :], swap).then_inc(shuf_ready, 1)

            def sine(t):
                dve.wait_ge(shuf_ready, t + 1)
                v = qksw[:, :, :, :].rearrange("p a s (b n) -> p (a s b) n", n=L)
                nc.vector.tensor_tensor(v, v, col(C_SIN, L).unsqueeze(1).broadcast_to([128, 4 * HB, L]),
                                        ALU.mult).then_inc(sin_ready, 1)

            def rotated(t):
                dve.wait_ge(sin_ready, t + 1)
                dve.wait_ge(cos_ready, t + 1)
                if t == 1:
                    dve.wait_ge(qbd_act, (8 - QD) * MC)
                nc.vector.tensor_tensor(qrot[:, :, :], qksw[:, 0, :, :], qkc[:, 0, :, :],
                                        ALU.add).then_inc(qrot_ready, 1)
                nc.vector.tensor_tensor(ke[:, :, t * HB:(t + 1) * HB, 0:L],
                                        qksw[:, 1, :, :].rearrange("p s (b n) -> p s b n", n=L),
                                        qkc[:, 1, :, :].rearrange("p s (b n) -> p s b n", n=L),
                                        ALU.add).then_inc(krot_ready, 1)

            def block_diagonal(t, s):
                dve.wait_ge(qrot_ready, t + 1)
                if t == 1:
                    dve.wait_ge(score_done, 2 * (s + 1))
                for h in range(QD):
                    nc.vector.tensor_scalar(qbd[:, s, :, h * L:(h + 1) * L],
                                            qrot[:, s, :].rearrange("p (b n) -> p b n", n=L),
                                            col(C_QM + h, 1), None, ALU.mult).then_inc(qbd_dve, 1)

            def softmax_top(st):
                x = sc[:, st % DEPTH, :, :]
                dve.wait_ge(z_in[st], 16)
                dve.wait_ge(score_copied, 2 * (st + 1))
                nc.vector.tensor_tensor(x, x, rl[:, st % DEPTH, :, :], ALU.add).then_inc(sum_ready, 1)
                dve.wait_ge(sum_ready, st + 1)
                nc.vector.tensor_reduce(st_mx[:, :], x, AX_X, ALU.max).then_inc(max_ready, 1)
                dve.wait_ge(max_ready, st + 1)
                nc.vector.tensor_tensor(x, x, st_mx[:, :].unsqueeze(2).broadcast_to([HR, CH, L]),
                                        ALU.subtract).then_inc(shift_ready, 1)

            def softmax_bottom(st):
                dve.wait_ge(exp_ready, st + 1)
                nc.vector.tensor_reduce(st_sum[:, st % 2, :], sc[:, st % DEPTH, :, :], AX_X,
                                        ALU.add).then_inc(den_ready, 1)
                dve.wait_ge(den_ready, st + 1)
                if st >= DEPTH:
                    dve.wait_ge(prob_ready, st - DEPTH + 1)
                nc.vector.reciprocal(st_inv[:, st % DEPTH, :], st_sum[:, st % 2, :]).then_inc(inv_ready, 1)

            def turn_copy(st, i):
                u = st * IPS + i
                dve.wait_ge(tr_done, u + 1)
                if st == 0:
                    dve.wait_ge(v_moved, 3 * 16)
                if st >= 2:
                    dve.wait_ge(ctx_done, st - 1)
                nc.vector.tensor_copy(pt[:, st % 2, i, :], ps[0:PAIR, u % 2, 0:IW]).then_inc(pt_odd, 1)

            def context_add(st):
                t, s, b0 = where(st)
                dve.wait_ge(ctx_half, st + 1)
                nc.vector.scalar_tensor_tensor(
                    out=ctxT[:, s, b0 * L:(b0 + IPS) * L].rearrange("p (i q) -> p i q", q=L),
                    in0=ps[:, 2 + st % 2, 0:IPS * PAIR].rearrange("p (i k) -> p i k", k=PAIR)[:, :, L:PAIR],
                    scalar=col(C_OM + 1, 1), in1=cth[:, st % 2, :, :],
                    op0=ALU.mult, op1=ALU.add).then_inc(ctx_ready, 1)

            def residual(t, bank):
                for m in range(MC):
                    dve.wait_ge(wo_done, 2 * t + m + 1)
                    nc.vector.tensor_tensor(hT[:, m, half(t)], hT[:, m, half(t)], ps[:, bank + m, 0:TH],
                                            ALU.add).then_inc(h2_ready, 1)

            def normalise(t):
                nc.vector.tensor_tensor(xn[:, :, half(t)], dT[:, :, half(t)],
                                        rs[:, half(t)].unsqueeze(1).broadcast_to([128, MC, TH]),
                                        ALU.mult).then_inc(xn_ready, 1)

            def split_x(t):
                dve.wait_ge(xhi_ready, t + 1)
                nc.vector.tensor_tensor(xlo[:, :, half(t)], xn[:, :, half(t)],
                                        xhi[:, :, half(t)].bitcast(F32), ALU.subtract).then_inc(xlo_ready, 1)

            def split_low(n, slot, slot_free=None):
                dve.wait_ge(whi_ready, n + 1)
                if slot_free is not None:
                    dve.wait_ge(down_done, slot_free)
                nc.vector.tensor_tensor(wlo[:, slot, :], wst[:, slot, :], whi[:, slot, :].bitcast(F32),
                                        ALU.subtract).then_inc(wlo_ready, 1)

            divide(0)
            shuffle(0)
            embed(1)
            sine(0)
            centre(0, 1, 1)
            rotated(0)
            block_diagonal(0, 0)
            divide(1)
            block_diagonal(0, 1)
            shuffle(1)
            sine(1)
            softmax_top(0)
            rotated(1)
            softmax_bottom(0)
            block_diagonal(1, 0)
            softmax_top(1)
            block_diagonal(1, 1)
            for st in range(2, DEPTH):
                softmax_bottom(st - 1)
                if st < DEPTH - 1:
                    softmax_top(st)
            for i in range(LEAD, NSTEP):
                turn_copy(i - LEAD, 1)
                softmax_top(i - LAG)
                turn_copy(i - LEAD, 3)
                softmax_bottom(i - LAG)
                if i > LEAD:
                    context_add(i - LEAD - 1)
            for st in range(NSTEP - LEAD, NSTEP + 1):
                context_add(st - 1)
                if st <= SPH:
                    softmax_top(st + LEAD - LAG)
                    softmax_bottom(st + LEAD - LAG)
                elif st == SPH + 1:
                    residual(0, 4)
                    centre(1, 0, 6)
                elif st < NSTEP:
                    turn_copy(st, 1)
                    turn_copy(st, 3)
                if st == NSTEP - 1:
                    deviation(1, 0)
            normalise(0)

            def gate_times_up(u, pair, r, ring_free=None):
                dve.wait_ge(silu_ready, u + 1)
                dve.wait_ge(up_done, u + 1)
                if ring_free is not None:
                    dve.wait_ge(act_ready, ring_free)
                nc.vector.tensor_tensor(gu[:, r, :], sg[:, pair, :], ps[:, 2 * pair + 1, 0:TH],
                                        ALU.mult).then_inc(gu_ready, 1)

            def act_low(u, r, ring_free=None):
                dve.wait_ge(ahi_ready, u + 1)
                if ring_free is not None:
                    dve.wait_ge(down_done, ring_free)
                nc.vector.tensor_tensor(alo[:, r, :], ac[:, r, :], ahi[:, r, :].bitcast(F32),
                                        ALU.subtract).then_inc(alo_ready, 1)

            count = [0]

            def routed(ins):
                count[0] += 1
                ins.then_inc(route, 1)
                dve.wait_ge(route, count[0])

            def route_groups():
                dve.wait_ge(sig_ready, 1)
                routed(nc.vector.tensor_tensor(g_sc[:, :, :], g_s[:, :, :],
                                               cs[0:PAIR, C_GB:C_GB + E].unsqueeze(1).broadcast_to([PAIR, NT, E]),
                                               ALU.add))
                q = g_sc[:, :, :].rearrange("p t (g e) -> p (t g) e", e=GE)
                nc.vector.tensor_tensor(g_pair[:, :, 0:3], q[:, :, 0:3], q[:, :, 1:4], ALU.add)
                nc.vector.tensor_tensor(g_pair[:, :, 3:5], q[:, :, 0:2], q[:, :, 2:4], ALU.add)
                routed(nc.vector.tensor_tensor(g_pair[:, :, 5:6], q[:, :, 0:1], q[:, :, 3:4], ALU.add))
                routed(nc.vector.tensor_reduce(g_gs[:, :, :].rearrange("p t g -> p (t g)"), g_pair[:, :, :],
                                               AX_X, ALU.max))

            def route_masked():
                for i in range(NT):
                    ins = nc.vector.max(g_gtop[:, i, :], g_gs[:, i, :])
                routed(ins)
                routed(nc.vector.memset(g_gtop[:, :, TKG:G], 3e38))
                for i in range(NT):
                    ins = nc.vector.match_replace(g_grep[:, i, :], g_gtop[:, i, :], g_gs[:, i, :], -3e38)
                routed(ins)
                routed(nc.vector.tensor_tensor(g_gm[:, :], g_grep[:, :, :].rearrange("p t g -> p (t g)"),
                                               g_gs[:, :, :].rearrange("p t g -> p (t g)"), ALU.not_equal))
                routed(nc.vector.tensor_tensor(g_mk[:, :, :].rearrange("p t (g e) -> p (t g) e", e=GE),
                                               g_sc[:, :, :].rearrange("p t (g e) -> p (t g) e", e=GE),
                                               g_gm[:, :].unsqueeze(2).broadcast_to([PAIR, NT * G, GE]), ALU.mult))

            def route_top():
                for i in range(NT):
                    ins = nc.vector.max(g_top[:, i, :], g_mk[:, i, :])
                routed(ins)
                for i in range(NT):
                    ins = nc.vector.match_replace(g_rep[:, i, :], g_top[:, i, :], g_mk[:, i, :], -3e38)
                routed(ins)

            def route_weights():
                routed(nc.vector.tensor_tensor(g_sel[:, :, :], g_rep[:, :, :], g_mk[:, :, :], ALU.not_equal))
                routed(nc.vector.tensor_tensor(g_w[:, :, :], g_s[:, :, :], g_sel[:, :, :], ALU.mult))
                routed(nc.vector.tensor_reduce(g_sum[:, :], g_w[:, :, :], AX_X, ALU.add))
                routed(nc.vector.tensor_scalar(g_sum[:, :], g_sum[:, :], 1e-20, None, ALU.add))
                routed(nc.vector.reciprocal(g_inv[:, :], g_sum[:, :]))
                routed(nc.vector.tensor_scalar(g_inv[:, :], g_inv[:, :], SCALE, None, ALU.mult))
                nc.vector.tensor_tensor(g_cw[:, :, :], g_w[:, :, :],
                                        g_inv[:, :].unsqueeze(2).broadcast_to([PAIR, NT, E]),
                                        ALU.mult).then_inc(comb_ready, 1)

            residual(1, 2)
            split_x(0)
            centre(1, 1, 6)
            deviation(1, 1)
            normalise(1)
            gate_times_up(0, 0, 0)
            gate_times_up(1, 1, 1)
            split_x(1)
            route_groups()
            route_masked()
            gate_times_up(2, 0, 2)
            gate_times_up(3, 1, 3)
            route_top()
            gate_times_up(4, 0, 0, 1)
            route_weights()
            gate_times_up(5, 1, 1, 2)
            gate_times_up(6, 0, 0, 3)
            split_low(RING, 0, 3)
            gate_times_up(7, 1, 1, 4)
            for t in range(2):
                act_low(2 * NSH + t, t, t + 1)

            def expert(n, slot, last):
                if not last:
                    split_low(n + 1, (slot + 1) % RING, 2 * (n + 1 - RING) + 2)
                for t in range(2):
                    u = 2 * n + t
                    gate_times_up(u, t, (2 * slot + t) % RING, u - 1)
                    act_low(u - 2, (2 * slot + 2 + t) % RING, u - 2 - RING + 1)

            with dve.Fori(0, (NE - 2 - RING) // RING) as turn_of_ring:
                n0 = turn_of_ring * RING + RING
                for k in range(RING):
                    expert(n0 + k, k, False)
            for n in range(NE - 2, NE):
                expert(n, n % RING, n == NE - 1)
            for t in range(2):
                u = 2 * (NE - 1) + t
                act_low(u, u % RING, u - RING + 1)
            for t in range(2):
                dve.wait_ge(down_done, 2 * NE - 1 + t)
                for m in range(MC):
                    nc.vector.tensor_tensor(oT[:, m, half(t)], hT[:, m, half(t)], ps[:, 4 + 2 * t + m, 0:TH],
                                            ALU.add).then_inc(out_ready, 1)

        @block.scalar
        def _(act):
            act.dma_start(cs[:, :], cst).then_inc(cst_in, 16)
            for c in range(1, KP, 2):
                act.dma_start(em[:, c, 0:D + TP], emb[c][:, 0:D + TP]).then_inc(em_in[c], 16)
            for c in range(1, KP, 2):
                act.dma_start(em[:, c, D + TP:D + 2 * TP], emb[c][:, D + TP:D + 2 * TP]).then_inc(em2_in[c], 16)
            act.dma_start(ve[L:PAIR, :, :], rel_v.unsqueeze(1).broadcast_to([L, B, D])).then_inc(relv_in, 16)

            def squares(k, t):
                act.wait_ge(d_ready, 2 * k + t + 1)
                nc.scalar.activation(xn[:, :, half(t)], dT[:, :, half(t)], ACT.Square).then_inc(sq_ready, 1)

            def root(k, t, bank):
                act.wait_ge(var_done, 2 * k + t + 1)
                nc.scalar.activation(sd[:, half(t)], ps[:, bank, 0:TH], ACT.Sqrt,
                                     bias=col(C_EPS, 1)).then_inc(sd_ready, 1)

            def load_table(k, function):
                nc.scalar.activation(warm[:, k:k + 1], col(C_EPS, 1), function).then_inc(warm_done, 1)

            act.wait_ge(cst_in, 16)
            load_table(0, ACT.Sqrt)
            squares(0, 0)
            root(0, 0, 0)
            squares(0, 1)

            def block_diagonal(t, s):
                act.wait_ge(qrot_ready, t + 1)
                if t == 1:
                    act.wait_ge(score_done, 2 * (s + 1))
                for h in range(QD, 8):
                    nc.scalar.activation(qbd[:, s, :, h * L:(h + 1) * L],
                                         qrot[:, s, :].rearrange("p (b n) -> p b n", n=L), ACT.Copy,
                                         scale=col(C_QM + h, 1)).then_inc(qbd_act, 1)

            def copy_scores(st):
                act.wait_ge(score_done, st + 1)
                if st >= DEPTH:
                    act.wait_ge(prob_ready, st - DEPTH + 1)
                    act.wait_ge(z_out[st - DEPTH], 16)
                src = ps[0:HR, score_banks(st):score_banks(st) + 2, 0:6 * PAIR].rearrange(
                    "p a (c k) -> p a c k", k=PAIR)
                for dst, k in ((zb, L), (sc, 0)):
                    nc.scalar.copy(dst[:, st % DEPTH, :, 0:L].rearrange("p (a c) k -> p a c k", a=2),
                                   src[:, :, :, k:k + L]).then_inc(score_copied, 1)
                    if dst is zb:
                        if st == 0:
                            act.wait_ge(zmask_ready, 1)
                        act.wait_ge(score_copied, 2 * st + 1)
                        act.dma_start(rows(zd, ZW, -1, st),
                                      zb[:, st % DEPTH, :, :].rearrange("p c k -> p (c k)")).then_inc(z_out[st], 16)

            def exponent(st):
                act.wait_ge(shift_ready, st + 1)
                nc.scalar.activation(sc[:, st % DEPTH, :, :], sc[:, st % DEPTH, :, :], ACT.Exp).then_inc(exp_ready, 1)

            def turn_copy(st, i):
                u = st * IPS + i
                act.wait_ge(tr_done, u + 1)
                if st == 0:
                    act.wait_ge(v_moved, 3 * 16)
                if st >= 2:
                    act.wait_ge(ctx_done, st - 1)
                nc.scalar.copy(pt[:, st % 2, i, :], ps[0:PAIR, u % 2, 0:IW]).then_inc(pt_odd if i % 2 else pt_even, 1)

            def context_half(st):
                act.wait_ge(ctx_done, st + 1)
                if st >= 2:
                    act.wait_ge(ctx_ready, st - 1)
                nc.scalar.activation(cth[:, st % 2, :, :],
                                     ps[:, 2 + st % 2, 0:IPS * PAIR].rearrange(
                                         "p (i k) -> p i k", k=PAIR)[:, :, 0:L],
                                     ACT.Copy, scale=col(C_OM, 1)).then_inc(ctx_half, 1)

            def split_x(t):
                act.wait_ge(xn_ready, 2 + t + 1)
                nc.scalar.copy(xhi[:, :, half(t)], xn[:, :, half(t)]).then_inc(xhi_ready, 1)

            def split_high(n, slot, slot_free=None):
                act.wait_ge(wt_in[slot], 4 * (n - slot) + 16)
                if slot_free is not None:
                    act.wait_ge(down_done, slot_free)
                nc.scalar.copy(whi[:, slot, :], wst[:, slot, :]).then_inc(whi_ready, 1)

            block_diagonal(0, 0)
            root(0, 1, 1)
            copy_scores(0)
            load_table(1, ACT.Exp)
            block_diagonal(0, 1)
            copy_scores(1)
            for k in range(6):
                if k == 4:
                    exponent(0)
                n = min(HR, T - k * HR)
                act.wait_ge(v_done, k // 2 + 1)
                nc.scalar.copy(vt[0:n, k, :], ps[0:n, k // 2, (k % 2) * D:(k % 2 + 1) * D]).then_inc(v_copied, 1)
            copy_scores(2)
            block_diagonal(1, 0)
            exponent(1)
            copy_scores(3)
            block_diagonal(1, 1)
            copy_scores(DEPTH)
            for n in range(2):
                split_high(n, n)
            exponent(2)
            for i in range(LEAD, NSTEP):
                turn_copy(i - LEAD, 0)
                if i == LEAD:
                    split_high(2, 2)
                else:
                    exponent(i - LAG)
                turn_copy(i - LEAD, 2)
                copy_scores(i)
                if i == LEAD:
                    exponent(i - LAG)
                    split_high(3, 3)
                else:
                    context_half(i - LEAD - 1)
            for st in range(NSTEP - LEAD, NSTEP + 1):
                context_half(st - 1)
                if st < NSTEP:
                    turn_copy(st, 0)
                    if st <= SPH + 1:
                        turn_copy(st, 1)
                    turn_copy(st, 2)
                    if st <= SPH + 1:
                        turn_copy(st, 3)
                    if st <= SPH:
                        exponent(st + LEAD - LAG)
                if st == SPH + 1:
                    load_table(2, ACT.Sqrt)
                    squares(1, 0)
                if st == SPH + 2:
                    root(1, 0, 7)
            split_x(0)

            def silu(u, pair, sg_free=None):
                act.wait_ge(gate_done, u + 1)
                if sg_free is not None:
                    act.wait_ge(gu_ready, sg_free)
                nc.scalar.activation(sg[:, pair, :], ps[:, 2 * pair, 0:TH], ACT.Silu).then_inc(silu_ready, 1)

            def act_high(u, r, ring_free=None):
                act.wait_ge(act_ready, u + 1)
                if ring_free is not None:
                    act.wait_ge(down_done, ring_free)
                nc.scalar.copy(ahi[:, r, :], ac[:, r, :]).then_inc(ahi_ready, 1)

            squares(1, 1)
            root(1, 1, 7)
            silu(0, 0)
            silu(1, 1)
            load_table(3, ACT.Sigmoid)
            split_x(1)
            act.wait_ge(logit_done, 2)
            nc.scalar.activation(g_s[:, :, :].rearrange("p t e -> p (t e)"), ps[0:PAIR, 6, 0:NT * E],
                                 ACT.Sigmoid).then_inc(sig_ready, 1)
            act_high(0, 0)
            act_high(1, 1)
            silu(2, 0, 1)
            silu(3, 1, 2)
            silu(4, 0, 3)
            silu(5, 1, 4)
            act_high(2, 2)
            act_high(3, 3)
            silu(6, 0, 5)
            act.wait_ge(combT_done, 1)
            for i in range(2):
                nc.scalar.copy(cT[:, half(i)], ps[0:E, 2 + i, 0:TH]).then_inc(combT_ready, 1)
            split_high(RING, 0, 3)
            act.wait_ge(row_done, 1)
            nc.scalar.copy(cb[:, NSH, :].rearrange("p (t n) -> p t n", t=2), ps[:, 0:2, 0:TH]).then_inc(row_ready, 1)
            silu(7, 1, 6)
            for t in range(2):
                act_high(2 * NSH + t, t, t + 1)

            def expert(n, slot, last):
                if not last:
                    split_high(n + 1, (slot + 1) % RING, 2 * (n + 1 - RING) + 2)
                for t in range(2):
                    u = 2 * n + t
                    silu(u, t, u - 1)
                    act_high(u - 2, (2 * slot + 2 + t) % RING, u - 2 - RING + 1)

            with act.Fori(0, (NE - 2 - RING) // RING) as turn_of_ring:
                n0 = turn_of_ring * RING + RING
                for k in range(RING):
                    expert(n0 + k, k, False)
            for n in range(NE - 2, NE):
                expert(n, n % RING, n == NE - 1)
            for t in range(2):
                u = 2 * (NE - 1) + t
                act_high(u, u % RING, u - RING + 1)

        @block.gpsimd
        def _(pool):
            nc.gpsimd.memset(zb[:, :, :, L:ZW], NEG).then_inc(zmask_ready, 1)
            pool.wait_ge(cst_in, 16)
            for s in range(MC):
                nc.gpsimd.tensor_copy(ke[:, s, :, L:PAIR],
                                      col(C_REL, L).unsqueeze(1).broadcast_to([128, B, L])).then_inc(ke_rel, 1)
            nc.gpsimd.memset(yb[:, :, :, :], 0.0).then_inc(y_zero, 1)

            def cosine(t):
                pool.wait_ge(qk_ready, 2 * t + 2)
                if t == 1:
                    pool.wait_ge(krot_ready, 1)
                nc.gpsimd.tensor_tensor(
                    qkc[:, :, :, :].rearrange("p a s (b n) -> p (a s b) n", n=L),
                    qk[:, :, :, :].rearrange("p a s (b n) -> p (a s b) n", n=L),
                    col(C_COS, L).unsqueeze(1).broadcast_to([128, 4 * HB, L]), ALU.mult).then_inc(cos_ready, 1)

            cosine(0)
            pool.wait_ge(proj_done, 2 * MC)
            nc.gpsimd.memset(qbd[:, :, :, 8 * L:IW], 0.0).then_inc(qbd_zero, 1)
            for t in range(2):
                pool.wait_ge(rs_ready, t + 1)
                nc.gpsimd.tensor_tensor(xn[:, :, half(t)], dT[:, :, half(t)],
                                        rs[:, half(t)].unsqueeze(1).broadcast_to([128, MC, TH]),
                                        ALU.mult).then_inc(xn_ready, 1)
                if t == 1:
                    cosine(1)

            pool.wait_ge(y_zero, 1)

            def probabilities(st):
                pool.wait_ge(inv_ready, st + 1)
                if st >= DEPTH:
                    pool.wait_ge(tr_done, IPS * (st - DEPTH + 1))
                nc.gpsimd.tensor_tensor(yb[:, st % DEPTH, :, L - 1:2 * L - 1], sc[:, st % DEPTH, :, :],
                                        st_inv[:, st % DEPTH, :].unsqueeze(2).broadcast_to([HR, CH, L]),
                                        ALU.mult).then_inc(prob_ready, 1)

            probabilities(0)
            for st in range(1, NSTEP):
                probabilities(st)
                n = st - 1
                if n < RING:
                    pool.wait_ge(whi_ready, n + 1)
                    nc.gpsimd.tensor_tensor(wlo[:, n, :], wst[:, n, :], whi[:, n, :].bitcast(F32),
                                            ALU.subtract).then_inc(wlo_ready, 1)

            pool.wait_ge(wo_done, 2 * MC)
            for n in range(NSH):
                nc.gpsimd.memset(cb[:, n, :], 1.0).then_inc(ones_ready, 1)
            pool.wait_ge(ones_ready, NSH)

            def weigh(u, r, slot, t, ring_free=None, made=None, place=None):
                made = u if made is None else made
                pool.wait_ge(gu_ready, made + 1)
                if ring_free is not None:
                    pool.wait_ge(ahi_ready, ring_free)
                    pool.wait_ge(alo_ready, ring_free)
                nc.gpsimd.tensor_tensor(ac[:, r, :], gu[:, r if place is None else place, :], cb[:, slot, half(t)],
                                        ALU.mult).then_inc(act_ready, 1)

            for t in range(2):
                for n in range(NSH):
                    u = NSH * t + n
                    weigh(u, u, n, t, made=n + RING * t, place=n)
                    pool.wait_ge(ahi_ready, u + 1)
                    nc.gpsimd.tensor_tensor(alo[:, u, :], ac[:, u, :], ahi[:, u, :].bitcast(F32),
                                            ALU.subtract).then_inc(alo_ready, 1)
            for n in range(NSH, RING):
                if n == NSH:
                    pool.wait_ge(row_ready, 1)
                else:
                    pool.wait_ge(cb_in[n], 16)
                for t in range(2):
                    u = 2 * n + t
                    weigh(u, u % RING, n, t, u - RING + 1, made=n + RING * t, place=(n, n - NSH)[t])
            with pool.Fori(0, (NE - 2 - RING) // RING) as turn_of_ring:
                n0 = turn_of_ring * RING + RING
                for k in range(RING):
                    pool.wait_ge(cb_in[k], 4 * n0 if k <= NSH else 4 * n0 + 16)
                    for t in range(2):
                        u = 2 * (n0 + k) + t
                        weigh(u, (2 * k + t) % RING, k, t, u - RING + 1)
            for n in range(NE - 2, NE):
                pool.wait_ge(cb_in[n % RING], 16 * (n // RING))
                for t in range(2):
                    u = 2 * n + t
                    weigh(u, u % RING, n % RING, t, u - RING + 1)


def tables():
    inv = (1.0 / np.float32(10000.0) ** (np.arange(0, HD, 2, dtype=np.float32) / np.float32(HD))).astype(np.float32)
    ang = np.outer(np.arange(L, dtype=np.float32), inv).astype(np.float32)
    f = (np.arange(128) % HD) // 2
    cos = np.cos(ang)[:, f].T.astype(np.float32)
    sin = np.sin(ang)[:, f].T.astype(np.float32)
    sin = np.where((np.arange(128) % 2 == 0)[:, None], -sin, sin)
    first = (np.arange(128) % 32 < HD).astype(np.float32)
    pair = np.stack([first, 1 - first], 1)
    heads = (np.arange(128)[:, None] // HD == np.arange(128 // HD)[None, :]).astype(np.float32)
    return cos, sin, heads * np.float32(0.25), pair


def kernel(x, L0_tok_W, L0_tok_b, L0_tok_class_token, L0_tok_pos_embedding, L0_attn_w_q, L0_attn_w_k, L0_attn_w_v,
           L0_attn_w_o, L0_attn_rel_emb, L0_ffn_gate_w, L0_ffn_gate_bias, L0_ffn_w_gate, L0_ffn_w_up, L0_ffn_w_down,
           L0_ffn_sh_gate, L0_ffn_sh_up, L0_ffn_sh_down):
    import concourse.bacc as bacc
    from concourse.bass_utils import run_bass_kernel_spmd

    a = np.asarray
    P = 16
    pat = a(x).reshape(B, 3, 6, P, 6, P).transpose(1, 3, 5, 0, 2, 4).reshape(KP, 128, B * NP)
    wtok = a(L0_tok_W).T.reshape(KP, 128, D)
    emb = np.ascontiguousarray(np.concatenate([wtok, pat], axis=2))
    offs = np.clip(np.arange(L) - (L - 1), -32, 32) + 32
    rel = a(L0_attn_rel_emb)[offs]
    rel_v = np.ascontiguousarray(np.tile(rel, (1, D // HD)))
    cos, sin, heads, pair = tables()

    def cols(v):
        return v.reshape(-1, MC, 128).transpose(2, 1, 0).reshape(128, -1)

    const = np.ascontiguousarray(np.concatenate([
        cols(a(L0_tok_b)), cols(a(L0_tok_class_token)), cols(a(L0_tok_pos_embedding)[0]), cos, sin,
        heads, pair, np.tile(rel.T, (128 // HD, 1)), cols(a(L0_ffn_gate_w)),
        np.broadcast_to(a(L0_ffn_gate_bias), (128, E)), np.full((128, 1), EPS), np.full((128, 128), 1 / D),
        np.eye(128)], axis=1), dtype=np.float32)
    wattn = np.ascontiguousarray(np.stack([a(w).T.reshape(MC, 128, D).transpose(1, 0, 2) for w in
                                           (L0_attn_w_q, L0_attn_w_k, L0_attn_w_v, L0_attn_w_o)], axis=1))

    def side(w):
        return w.reshape(-1, INTER, MC, 128).transpose(0, 3, 2, 1).reshape(-1, 128, D)

    wexp = np.ascontiguousarray(np.concatenate([
        np.concatenate([side(a(L0_ffn_sh_gate)), side(a(L0_ffn_w_gate))]),
        np.concatenate([side(a(L0_ffn_sh_up)), side(a(L0_ffn_w_up))]),
        np.concatenate([a(L0_ffn_sh_down).reshape(D, NSH, INTER).transpose(1, 2, 0),
                        a(L0_ffn_w_down).transpose(0, 2, 1)])], axis=2))

    nc = bacc.Bacc("TRN2", target_bir_lowering=False, num_devices=1)
    arrays = {"emb": emb, "cst": const, "rel_v": rel_v, "wattn": wattn, "wexp": wexp}
    aps = [nc.dram_tensor(n, v.shape, F32, kind="ExternalInput").ap() for n, v in arrays.items()]
    aps.append(nc.dram_tensor("out", (MC, 128, T), F32, kind="ExternalOutput").ap())
    build(nc, *aps)
    r = run_bass_kernel_spmd(nc, [arrays], core_ids=[0])
    return np.ascontiguousarray(r.results[0]["out"].reshape(MC, 128, B, L).transpose(2, 3, 0, 1).reshape(B, L, D))
```
